# Optimizing a Trainium2 kernel written in Bass

```python
import numpy as np
import jax
import jax.numpy as jnp

def _softmax(x, axis=-1):
    return jax.nn.softmax(x, axis=axis)

def _gelu(x):
    return jax.nn.gelu(x, approximate=True)

def _silu(x):
    return jax.nn.silu(x)

def _sigmoid(x):
    return jax.nn.sigmoid(x)

def _layernorm(x, axis=-1, eps=1e-05):
    m = jnp.mean(x, axis=axis, keepdims=True)
    v = jnp.var(x, axis=axis, keepdims=True)
    return (x - m) / jnp.sqrt(v + eps)

def _scatter_add(tgt, idx, src, axis=0):
    return tgt.at[idx].add(src)

def _segment_sum(src, seg, n):
    return jax.ops.segment_sum(src, seg, n)
kernel_name = 'mk_gnn_resnorm_d1_gnn_r32_838e1e'

def setup_inputs(seed: int=0):
    np.random.seed(seed)
    _w = jnp.asarray

    def _rec_inputs():
        import jax
        import jax.numpy as jnp
        _gk = jax.random.key(seed)
        x = -0.0008691 + 1 * jax.random.normal(jax.random.fold_in(_gk, 1), (50000, 128), jnp.float32)
        src = jax.random.randint(jax.random.fold_in(_gk, 2), (25000,), 0, 50000, jnp.int32)
        dst = jnp.minimum((50000 * jax.random.uniform(jax.random.fold_in(_gk, 3), (25000,)) ** 2.0).astype(jnp.int32), 49999)
        _o = jnp.argsort(dst, stable=True)
        src = src[_o]
        dst = dst[_o]
        edge_attr_16 = -0.000191324 + 0.999809 * jax.random.normal(jax.random.fold_in(_gk, 11), (25000, 16), jnp.float32)
        return (x, src, dst, edge_attr_16)
    x, src, dst, edge_attr_16 = _rec_inputs()

    def _L0_gnn_setup():
        import jax, jax.numpy as jnp
        import numpy as np
        N_NODES = 10000
        N_EDGES = 10000
        IN_CH = 128
        LAYER = 128
        EDGE_DIM = 16

        def _edge_conv(x, src, dst, edge_attr, W, b, denom):
            msg = jnp.concatenate([x[src], edge_attr], axis=1) @ W + b
            s = jax.ops.segment_sum(msg, dst, num_segments=x.shape[0])
            return s / denom[:, None]
        key = jax.random.key(seed)
        ks = jax.random.split(key, 12)

        def w(k, shp):
            fan_in = shp[0]
            return jax.random.normal(k, shp, dtype=jnp.float32) / jnp.sqrt(jnp.float32(fan_in))
        return {'x': jax.random.normal(ks[0], (N_NODES, IN_CH), dtype=jnp.float32), 'edge_attr': jax.random.normal(ks[1], (N_EDGES, EDGE_DIM), dtype=jnp.float32), 'edge_index': jax.random.randint(ks[2], (2, N_EDGES), 0, N_NODES, dtype=jnp.int32), 'W0': w(ks[3], (IN_CH + EDGE_DIM, LAYER)), 'b0': jnp.zeros((LAYER,), jnp.float32), 'W1': w(ks[4], (LAYER + EDGE_DIM, LAYER)), 'b1': jnp.zeros((LAYER,), jnp.float32), 'W2': w(ks[5], (2 * LAYER + EDGE_DIM, LAYER)), 'b2': jnp.zeros((LAYER,), jnp.float32), 'W3': w(ks[6], (3 * LAYER + EDGE_DIM, LAYER)), 'b3': jnp.zeros((LAYER,), jnp.float32)}
    _L0_gnn_all = _L0_gnn_setup()
    _L0_gnn_in = {k: v for k, v in _L0_gnn_all.items() if k in ('W0', 'b0', 'W1', 'b1', 'W2', 'b2', 'W3', 'b3')}
    del _L0_gnn_all
    return {'x': x, 'src': src, 'dst': dst, 'edge_attr_16': edge_attr_16, 'L0_gnn_W0': _L0_gnn_in['W0'], 'L0_gnn_b0': _L0_gnn_in['b0'], 'L0_gnn_W1': _L0_gnn_in['W1'], 'L0_gnn_b1': _L0_gnn_in['b1'], 'L0_gnn_W2': _L0_gnn_in['W2'], 'L0_gnn_b2': _L0_gnn_in['b2'], 'L0_gnn_W3': _L0_gnn_in['W3'], 'L0_gnn_b3': _L0_gnn_in['b3']}

def reference(x, src, dst, edge_attr_16, L0_gnn_W0, L0_gnn_b0, L0_gnn_W1, L0_gnn_b1, L0_gnn_W2, L0_gnn_b2, L0_gnn_W3, L0_gnn_b3):
    import jax
    import jax.numpy as jnp

    def _L0_gnn_ref(x, edge_attr, edge_index, W0, b0, W1, b1, W2, b2, W3, b3):
        import jax, jax.numpy as jnp
        import numpy as np
        N_NODES = 10000
        N_EDGES = 10000
        IN_CH = 128
        LAYER = 128
        EDGE_DIM = 16

        def _edge_conv(x, src, dst, edge_attr, W, b, denom):
            msg = jnp.concatenate([x[src], edge_attr], axis=1) @ W + b
            s = jax.ops.segment_sum(msg, dst, num_segments=x.shape[0])
            return s / denom[:, None]
        src, dst = (edge_index[0], edge_index[1])
        counts = jax.ops.segment_sum(jnp.ones((src.shape[0],), x.dtype), dst, num_segments=x.shape[0])
        denom = jnp.maximum(counts, 1.0)
        h = _edge_conv(x, src, dst, edge_attr, W0, b0, denom)
        outputs = [h]
        for W, b in ((W1, b1), (W2, b2), (W3, b3)):
            cat = jnp.concatenate(outputs, axis=1)
            z = _edge_conv(cat, src, dst, edge_attr, W, b, denom)
            outputs.append(z)
        return outputs[-1]
    edge_index = jnp.stack([src, dst])
    x = _layernorm(x + _L0_gnn_ref(x, edge_attr_16, edge_index, L0_gnn_W0, L0_gnn_b0, L0_gnn_W1, L0_gnn_b1, L0_gnn_W2, L0_gnn_b2, L0_gnn_W3, L0_gnn_b3), axis=-1)
    return x

_drawn_inputs = setup_inputs


def setup_inputs(seed=0):
    import zlib

    import numpy as np

    out = dict(_drawn_inputs(seed))
    spreads = {'L0_gnn_b0': (0.0, 0.415),
     'L0_gnn_b1': (0.0, 0.477),
     'L0_gnn_b2': (0.0, 0.525),
     'L0_gnn_b3': (0.0, 0.1)}
    factors = {}
    for name, (base, spread) in spreads.items():
        noise = np.random.default_rng([zlib.crc32(name.encode()), seed]).standard_normal(out[name].shape)
        drawn = base * np.exp(spread * noise) if base else spread * noise
        out[name] = jnp.asarray(drawn.astype(out[name].dtype))
    for name, factor in factors.items():
        out[name] = (out[name] * factor).astype(out[name].dtype)
    return out
```

```python
import concourse.bass as bass
from concourse import mybir
from concourse.alu_op_type import AluOpType as ALU
from contextlib import ExitStack

P = 128
N, D, E, DE = 50000, 128, 25000, 16
T = (E + P - 1) // P
HALF = 7
BODY = 2 * HALF
IT = T // BODY
CT = 200
CG = 4
CW = CG * P
CIT = CT // (2 * CG)
NSEG = CT * P
HI = (N + P - 1) // P
EW = DE + 3
EP = 3 * DE + 3
LR = 5
LIT = N // (P * LR * 2)
LREST = N - LIT * 2 * LR * P
EPS = 1e-5
f32, bf16, f16 = mybir.dt.float32, mybir.dt.bfloat16, mybir.dt.float16
i32, u32 = mybir.dt.int32, mybir.dt.uint32
ACT = mybir.ActivationFunctionType
AX = mybir.AxisListType


class Chain:

    def __init__(self, eng, sem):
        self.eng, self.sem, self.base, self.n = eng, sem, 0, 0

    def __call__(self, ins):
        self.n += 1
        ins.then_inc(self.sem, 1)
        self.eng.wait_ge(self.sem, self.base + self.n)

    def loop(self, i, per):
        self.start, self.per = self.base + self.n, per
        self.base, self.n = i * per + self.start, 0

    def end(self, count):
        assert self.n == self.per, self.n
        self.base, self.n = self.start + count * self.per, 0


def gnn_kernel(nc, x, dst_t, prev_t, src_t, src_rows, ea, wx, we, out):
    H = [nc.dram_tensor(f"h{k}_rows", [NSEG + 1, D], f32).ap() for k in range(3)]
    UD = [nc.dram_tensor(f"u{k}_cols", [P, NSEG], f32).ap() for k in (1, 2)]
    ETD = nc.dram_tensor("edge_sum_cols", [DE + 1, NSEG], f32).ap()

    with ExitStack() as ctx:
        sb = lambda n, s, d: ctx.enter_context(nc.sbuf_tensor(n, s, d))
        pb = lambda n: ctx.enter_context(nc.psum_tensor(n, [P, 512], f32))
        sem = lambda n: ctx.enter_context(nc.semaphore(n))

        UT = sb("UT", [P, NSEG], f32)
        EC = sb("EC", [P, CT * EW], f32)
        ECv = EC[:, :].rearrange("p (c w) -> p c w", w=EW)
        G = sb("G", [P, BODY, D], f32)
        S = sb("S", [P, HALF, P], f32)
        SA = sb("SA", [P, HALF, 2 * P], bf16)
        EF = sb("EF", [P, 2, HALF, DE], f32)
        EB = sb("EB", [P, 2, HALF, EP], bf16)
        ECS = sb("ECS", [P, 2, CG, EW], f32)
        OH = sb("OH", [P, 2, HI + 1], f16)
        LA = sb("LA", [P, 2, 2, P], f16)
        TAB = sb("TAB", [P, 2, HI + 1], f16)
        TABI = sb("TABI", [P, 2, HI + 1], i32)
        ZH = sb("ZH", [P, HI + 1], f16)
        WX = sb("WX", [P, 7, D], f32)
        WE = sb("WE", [P, 4, D], f32)
        US = sb("US", [P, 2, CW], f32)
        U1 = sb("U1", [P, 2, CW], f32)
        U2 = sb("U2", [P, 2, CW], f32)
        ET = sb("ET", [P, 2, CW], f32)
        HS = sb("HS", [P, 2, CW], f32)
        ZERO = sb("ZERO", [P, CW], f32)
        ident = sb("ident", [P, P], f32)
        tri = sb("tri", [P, P], bf16)
        ones = sb("ones", [P, P], bf16)
        row0 = sb("row0", [P, P], bf16)
        iota = sb("iota", [P, 2 * P], f32)
        iotah = sb("iotah", [P, HI + 1], f16)
        iotap = sb("iotap", [P, 1], f32)
        eps = sb("eps", [P, 1], f32)
        dsti = sb("dsti", [P, T], i32)
        previ = sb("previ", [P, T], i32)
        srci = sb("srci", [P, T], i32)
        ti = sb("ti", [P, CT], i32)
        seg = sb("seg", [P, T], f32)
        rel = sb("rel", [P, T], f32)
        rela = sb("rela", [P, T], f32)
        nh = sb("nh", [P, T], f32)
        nl = sb("nl", [P, T], f32)
        first = sb("first", [P, T], bf16)
        idx = sb("idx", [P, T], f32)
        s0r = sb("s0r", [P, T], i32)
        c0r = sb("c0r", [P, T], i32)
        nodes = sb("nodes", [P, CT], f32)
        nodec = sb("nodec", [P, CT], f32)
        inv = sb("inv", [P, CT], f32)
        istage = sb("istage", [P, 2, HALF], u32)
        nstage = sb("nstage", [P, 2, 2 * CG], u32)
        stat = sb("stat", [P, 2, LR, 6], f32)
        mv = sb("mv", [P, 2, LR, 2], f32)
        sd = sb("sd", [P, 2, LR], f32)
        rs = sb("rs", [P, 2, LR], f32)
        XL = sb("XL", [P, 2, LR * D], f32)
        SLO = sb("SLO", [P, 2, HALF * P], i32)
        JUNK = sb("JUNK", [P, 2, HI + 1], f32)
        OS = sb("OS", [P, 2, HALF * P], f16)
        nlo, nhi, wlo, whi, shi = (sb(n, [P, CT], f32) for n in ("nlo", "nhi", "wlo", "whi", "shi"))

        SG = [pb("segp0"), pb("segp1")]
        LP = [pb("lp0"), pb("lp1")]
        TP = pb("tp")
        HP = [pb("hp0"), pb("hp1")]

        names = ("ld_dst ld_prev ld_src ld_w const dve prep_in prep_mm prep_done zrow "
                 "idx_ready s_built summed added e_added e_split e_built ecs_full et_mm et_copied ec_ready "
                 "oh_built tab_mm tab_ready os_built look_mm looked us_staged h_mm h_read ut_zero "
                 "n_staged f_add f_stat f_sd f_out ln_stat ln_sd ln_done tick pool_tick").split()
        s = {n: sem(n) for n in names}
        gat = [sem(f"gathered{j}") for j in range(BODY)]
        two = lambda n: [sem(f"{n}{b}") for b in (0, 1)]
        ld_ea, ld_lo, st_et, ld_et, ld_u1, ld_u2, st_u, st_h, ld_x, st_o = (
            two(n) for n in "ld_ea ld_lo st_et ld_et ld_u1 ld_u2 st_u st_h ld_x st_o".split())
        scat = [sem(f"scattered{j}") for j in range(2 * CG)]
        xg = [sem(f"x_gathered{j}") for j in range(2 * CG)]
        block = ctx.enter_context(nc.Block())

        hrows = [h[1:NSEG + 1, :].rearrange("(g j p) c -> g p j c", p=P, j=CG) for h in H]
        xv = x[0:LIT * 2 * LR * P, :].rearrange("(g p r) c -> g p (r c)", p=P, r=LR)
        ov = out[0:LIT * 2 * LR * P, :].rearrange("(g p r) c -> g p (r c)", p=P, r=LR)
        one = lambda ap, g: ap[bass.ds(g, 1)]
        NG = 2 * CIT

        @block.sync
        def _(e):
            e.dma_start(dsti[:, :], dst_t).then_inc(s["ld_dst"], 16)
            e.dma_start(previ[:, :], prev_t).then_inc(s["ld_prev"], 16)
            e.dma_start(WX[:, :, :], wx).then_inc(s["ld_w"], 16)
            e.wait_ge(s["const"], 1)
            e.dma_start(WE[0:DE + 1, :, :], we).then_inc(s["ld_w"], 16)
            for k in range(3):
                e.dma_start(H[k][0:1, :], ZERO[0:1, 0:D]).then_inc(s["zrow"], 16)
            for b in (0, 1):
                e.sem_inc(st_et[b], 16)
                e.sem_inc(st_u[b], 16)
                e.sem_inc(st_h[b], 16)
            with e.Fori(0, IT) as i:
                for b in (0, 1):
                    h = i * 2 + b
                    e.wait_ge(s["e_split"], h + 1)
                    e.dma_start(EF[:, b, :, :], one(ea, h).rearrange("o p j w -> (o p) j w")).then_inc(ld_ea[b], 16)
            with e.Fori(0, CIT) as i:
                for b in (0, 1):
                    g = i * 2 + b
                    e.wait_ge(s["et_copied"], g + 3)
                    e.dma_start(ETD[:, bass.ds(g * CW, CW)], ET[0:DE + 1, b, :]).then_inc(st_et[b], 16)
            with e.Fori(0, IT) as i:
                for b in (0, 1):
                    h = i * 2 + b
                    e.wait_ge(s["os_built"], h + 1)
                    e.dma_start(SLO[:, b, :], src_rows[bass.ds(h * HALF * P, HALF * P)].partition_broadcast(P)).then_inc(ld_lo[b], 16)
            for b in (0, 1):
                e.wait_ge(st_et[b], 16 * (CIT + 1))
            for k in range(4):
                if k == 1:
                    with e.Fori(0, LIT) as i:
                        for b in (0, 1):
                            g = i * 2 + b
                            e.wait_ge(s["ln_done"], g + 1)
                            e.wait_ge(st_o[b], i * 16 + 16)
                            e.dma_start(XL[:, b, :], one(xv, g).rearrange("o p w -> (o p) w")).then_inc(ld_x[b], 16)
                    e.wait_ge(s["ln_done"], 2 * LIT + 1)
                    e.wait_ge(st_o[0], 16 * (LIT + 1))
                    e.dma_start(XL[0:LREST, 0, 0:D], x[N - LREST:N, :]).then_inc(ld_x[0], 16)
                if k >= 2:
                    for b in (0, 1):
                        e.wait_ge(st_u[b], 16 * (CIT * (k - 1) + 1))
                with e.Fori(0, CIT) as i:
                    for b in (0, 1):
                        g = i * 2 + b
                        cols = bass.ds(g * CW, CW)
                        e.wait_ge(s["h_mm"], g + (NG * k + 1))
                        e.dma_start(ET[0:DE + 1, b, :], ETD[:, cols]).then_inc(ld_et[b], 16)
                        if k >= 2:
                            e.dma_start(U1[:, b, :], UD[0][:, cols]).then_inc(ld_u1[b], 16)
                        if k == 3:
                            e.dma_start(U2[:, b, :], UD[1][:, cols]).then_inc(ld_u2[b], 16)
                    for b in (0, 1):
                        g = i * 2 + b
                        cols = bass.ds(g * CW, CW)
                        if k in (1, 2):
                            e.wait_ge(s["us_staged"], g + (NG * k + 1))
                            e.dma_start(UD[k - 1][:, cols], US[:, b, :]).then_inc(st_u[b], 16)
                        if k < 3:
                            e.wait_ge(s["h_read"], g + (NG * k + 3))
                            e.dma_start(one(hrows[k], g).rearrange("o p j c -> (o p) j c"),
                                        HS[:, b, :].rearrange("p (j c) -> p j c", c=D)).then_inc(st_h[b], 16)

        @block.gpsimd
        def _(e):
            g = nc.gpsimd
            g.memset(ZERO[:, :], 0.0)
            g.memset(WE[:, :, :], 0.0)
            g.memset(ET[:, :, :], 0.0).then_inc(s["const"], 1)
            g.memset(ones[:, :], 1.0)
            g.memset(ident[:, :], 0.0)
            g.memset(tri[:, :], 1.0)
            g.memset(row0[:, :], 1.0)
            g.memset(ZH[:, :], 0.0)
            g.memset(eps[:, :], EPS)
            g.memset(EB[:, :, :, DE:DE + 1], 1.0)
            g.iota(iota[:, :], [[1, 2 * P]], base=0, channel_multiplier=0, allow_small_or_imprecise_dtypes=True)
            g.iota(iotah[:, :], [[1, HI + 1]], base=0, channel_multiplier=0, allow_small_or_imprecise_dtypes=True)
            g.iota(ti[:, :], [[P, CT]], base=1, channel_multiplier=1)
            g.iota(iotap[:, :], [[0, 1]], base=0, channel_multiplier=1, allow_small_or_imprecise_dtypes=True).then_inc(s["const"], 1)
            e.wait_ge(s["const"], 2)
            g.affine_select(out=tri[:, :], in_=tri[:, :], compare_op=ALU.is_ge, fill=0.0, base=0, pattern=[[1, P]], channel_multiplier=-1)
            g.affine_select(out=row0[:, :], in_=row0[:, :], compare_op=ALU.is_equal, fill=0.0, base=0, pattern=[[0, P]], channel_multiplier=1)
            g.affine_select(out=ident[:, :], in_=ident[:, :], compare_op=ALU.not_equal, fill=1.0, base=0, pattern=[[1, P]], channel_multiplier=-1).then_inc(s["const"], 1)
            last_node = e.snap(e.to_reg(N - 1))
            last_row = e.snap(e.to_reg(NSEG))
            for k in range(4):
                table = x if k == 0 else H[k - 1]
                if k:
                    e.wait_ge(s["zrow"], 48)
                    for b in (0, 1):
                        e.wait_ge(st_h[b], 16 * (CIT * k + 1))
                with e.Fori(0, IT) as i:
                    for b in (0, 1):
                        e.wait_ge(s["idx_ready"], i * 2 + (b + 1 + 2 * IT * k))
                        e.wait_ge(s["summed"], i * BODY + ((b + 1) * HALF + T * k))
                        e.sem_inc(s["pool_tick"], 1)
                        for j in range(HALF):
                            slot = b * HALF + j
                            g.indirect_dma_start(G[:, slot, :], None, table,
                                                 bass.IndirectOffsetOnAxis(ap=istage[:, b, j:j + 1], axis=0),
                                                 bounds_check=last_row if k else last_node, oob_is_err=False).then_inc(gat[slot], 16)
            e.wait_ge(s["summed"], BODY + 4 * T)
            for b in (0, 1):
                e.wait_ge(st_o[b], 16 * (LIT + 1 + (b == 0)))
            with e.Fori(0, CIT) as i:
                for b in (0, 1):
                    gg = i * 2 + b
                    e.wait_ge(s["n_staged"], gg + 1)
                    e.wait_ge(s["f_add"], gg + 1)
                    e.sem_inc(s["pool_tick"], 1)
                    for j in range(CG):
                        q = b * CG + j
                        g.indirect_dma_start(G[:, q, :], None, x, bass.IndirectOffsetOnAxis(ap=nstage[:, b, j:j + 1], axis=0),
                                             bounds_check=last_node, oob_is_err=False).then_inc(xg[q], 16)
                for b in (0, 1):
                    gg = i * 2 + b
                    e.wait_ge(s["f_out"], gg + 1)
                    e.sem_inc(s["pool_tick"], 1)
                    for j in range(CG):
                        q = b * CG + j
                        g.indirect_dma_start(out, bass.IndirectOffsetOnAxis(ap=nstage[:, b, CG + j:CG + j + 1], axis=0),
                                             HS[:, b, j * D:(j + 1) * D], None,
                                             bounds_check=last_node, oob_is_err=False).then_inc(scat[q], 16)
            for q in range(2 * CG):
                e.wait_ge(scat[q], 16 * CIT)

        @block.scalar
        def _(e):
            a = nc.scalar

            def stage_indices(k, arr):
                with e.Fori(0, IT) as i:
                    for b in (0, 1):
                        e.wait_ge(s["summed"], (i * 2 + b) * HALF + (HALF + T * k))
                        a.copy(istage[:, b, :], arr[:, bass.ds((i * 2 + b) * HALF, HALF)]).then_inc(s["idx_ready"], 1)

            e.sem_inc(s["et_copied"], 2)
            for b in (0, 1):
                e.sem_inc(st_o[b], 16)
            e.dma_start(srci[:, :], src_t).then_inc(s["ld_src"], 16)
            e.wait_ge(s["ld_src"], 16)
            stage_indices(0, srci)
            e.wait_ge(s["ec_ready"], 1)
            with e.Fori(0, CIT) as i:
                for b in (0, 1):
                    g = i * 2 + b
                    e.wait_ge(s["et_mm"], g + 1)
                    a.copy(ECS[:, b, :, :], ECv[:, bass.ds(g * CG, CG), :]).then_inc(s["ecs_full"], 1)
                for b in (0, 1):
                    g = i * 2 + b
                    e.wait_ge(s["et_mm"], g + 3)
                    e.wait_ge(st_et[b], i * 16 + 16)
                    a.copy(ET[0:DE + 1, b, :], HP[b][0:DE + 1, :]).then_inc(s["et_copied"], 1)
            for k in range(4):
                if k:
                    if k == 1:
                        with e.Fori(0, LIT) as i:
                            for b in (0, 1):
                                g = i * 2 + b
                                e.wait_ge(s["ln_stat"], g + 1)
                                a.activation(sd[:, b, :], mv[:, b, :, 1], ACT.Sqrt, bias=eps[:, 0:1]).then_inc(s["ln_sd"], 1)
                            for b in (0, 1):
                                g = i * 2 + b
                                e.wait_ge(s["ln_done"], g + 3)
                                e.dma_start(one(ov, g).rearrange("o p w -> (o p) w"), XL[:, b, :]).then_inc(st_o[b], 16)
                        e.wait_ge(s["ln_stat"], 2 * LIT + 1)
                        a.activation(sd[0:LREST, 0, 0:1], mv[0:LREST, 0, 0:1, 1], ACT.Sqrt, bias=eps[0:LREST, 0:1]).then_inc(s["ln_sd"], 1)
                        e.wait_ge(s["ln_done"], 2 * LIT + 3)
                        e.dma_start(out[N - LREST:N, :], XL[0:LREST, 0, 0:D]).then_inc(st_o[0], 16)
                        e.wait_ge(s["looked"], 2 + T)
                    stage_indices(k, idx)
                e.wait_ge(s["added"], 2 + T * (k + 1))
                def stage(i, k, peeled=False):
                    for b in (0, 1):
                        g = i * 2 + b
                        e.wait_ge(s["h_mm"], g + (NG * k + 1))
                        if k in (1, 2):
                            e.wait_ge(st_u[b], i * 16 + (CIT * (k - 1) + 1) * 16)
                        if k == 3:
                            e.wait_ge(st_u[b], (CIT * 2 + 1) * 16)
                            if not peeled:
                                for q in range(CG):
                                    e.wait_ge(scat[b * CG + q], i * 16)
                            a.copy(nstage[:, b, 0:CG], nodec[:, bass.ds(g * CG, CG)])
                            a.copy(nstage[:, b, CG:2 * CG], nodes[:, bass.ds(g * CG, CG)]).then_inc(s["n_staged"], 1)
                        a.copy(US[:, b, :], UT[:, bass.ds(g * CW, CW)]).then_inc(s["us_staged"], 1)
                    if k == 3:
                        for b in (0, 1):
                            g = i * 2 + b
                            e.wait_ge(s["f_stat"], g + 1)
                            a.activation(sd[:, b, 0:CG], mv[:, b, 0:CG, 1], ACT.Sqrt, bias=eps[:, 0:1]).then_inc(s["f_sd"], 1)

                if k == 3:
                    stage(0, k, True)
                with e.Fori(1 if k == 3 else 0, CIT) as i:
                    stage(i, k)

        @block.vector
        def _(e):
            v = nc.vector
            link = Chain(e, s["dve"])
            for n in ("added", "e_added", "e_split", "looked", "h_read", "os_built", "f_add", "ln_done"):
                e.sem_inc(s[n], 2)
            v.memset(UT[:, :], 0.0)
            v.memset(EC[:, :], 0.0)
            e.wait_ge(s["ld_dst"], 16)
            e.wait_ge(s["ld_prev"], 16)
            e.wait_ge(s["const"], 3)
            v.tensor_scalar(ti[:, 0:1], ti[:, 0:1], 0, None, ALU.bitwise_or) if False else None
            link(v.tensor_tensor(first[:, :], dsti[:, :], previ[:, :], ALU.not_equal))
            v.tensor_copy(seg[:, :], first[:, :])
            e.wait_ge(s["dve"], link.n)
            v.tensor_scalar(s0r[:, :], dsti[:, :], 8, None, ALU.logical_shift_right)
            link(v.tensor_scalar(c0r[:, :], dsti[:, :], 255, None, ALU.bitwise_and))
            v.tensor_tensor(nh[:, :], s0r[:, :], seg[:, :], ALU.mult)
            link(v.tensor_tensor(nl[:, :], c0r[:, :], seg[:, :], ALU.mult))
            nc.vector.sem_inc(s["prep_in"], 1) if False else None
            link(v.tensor_copy(rel[:, :], first[:, :]))
            v.tensor_copy(rela[:, 0:1], first[:, 0:1]).then_inc(s["prep_in"], 1)
            e.wait_ge(s["prep_mm"], 1)
            link(v.tensor_copy(rela[:, :], LP[1][:, 0:T]))
            link(v.tensor_tensor_scan(seg[:, :], rela[:, :], rela[:, :], 0.0, ALU.add, ALU.bypass))
            link(v.tensor_tensor(seg[:, :], seg[:, :], rela[:, :], ALU.subtract))
            link(v.tensor_tensor(rela[:, :], seg[:, :], HP[0][:, 0:T], ALU.add))
            link(v.tensor_scalar(rela[:, :], rela[:, :], -1.0, None, ALU.add))
            link(v.tensor_copy(s0r[:, :], rela[:, :]))
            link(v.tensor_scalar(c0r[:, :], s0r[:, :], 7, None, ALU.logical_shift_right))
            link(v.tensor_tensor(seg[:, :], seg[:, :], LP[0][:, 0:T], ALU.add))
            link(v.tensor_scalar(seg[:, :], seg[:, :], -1.0, None, ALU.add))
            link(v.tensor_tensor(rel[:, :], seg[:, :], rela[:, :], ALU.subtract))
            link(v.tensor_copy(rela[:, :], c0r[:, :]))
            link(v.tensor_scalar(rela[:, :], rela[:, :], -float(P), None, ALU.mult))
            link(v.tensor_tensor(rela[:, :], seg[:, :], rela[:, :], ALU.add))
            link(v.tensor_copy(seg[:, :], c0r[:, :]))
            link(v.tensor_scalar(seg[:, :], seg[:, :], float(EW), None, ALU.mult))
            link(v.tensor_copy(c0r[:, :], seg[:, :]))
            srows = [e.alloc_register(f"win{j}") for j in range(HALF)]
            crows = [e.alloc_register(f"ewin{j}") for j in range(HALF)]

            def sums(k):
                PER = 4 if k == 0 else 0
                with e.Fori(0, IT) as i:
                    link.loop(i, 2 * PER)
                    for b in (0, 1):
                        h = i * 2 + b
                        if k == 0:
                            e.wait_ge(ld_ea[b], i * 16 + 16)
                        e.wait_ge(s["summed"], h * HALF + (BODY + T * k))
                        for j in range(HALF):
                            c = bass.ds(h * HALF + j, 1)
                            if k == 0:
                                v.tensor_scalar(SA[:, j, :], iota[:, :], rela[:, c], None, ALU.is_equal)
                            v.tensor_scalar(S[:, j, :], iota[:, 0:P], rel[:, c], None, ALU.is_equal).then_inc(s["s_built"], 1)
                        if k == 0:
                            hi_, mid, lo = (EB[:, b, :, w:w + DE] for w in (0, EW, EW + DE))
                            v.tensor_copy(EB[:, b, :, DE + 1], nh[:, bass.ds(h * HALF, HALF)])
                            v.tensor_copy(EB[:, b, :, DE + 2], nl[:, bass.ds(h * HALF, HALF)])
                            link(v.tensor_copy(hi_, EF[:, b, :, :]))
                            link(v.tensor_tensor(EF[:, b, :, :], EF[:, b, :, :], hi_, ALU.subtract))
                            link(v.tensor_copy(mid, EF[:, b, :, :]))
                            link(v.tensor_tensor(lo, EF[:, b, :, :], mid, ALU.subtract))
                            v.sem_inc(s["e_split"], 1)
                            v.sem_inc(s["e_built"], 1)
                        v.load(srows, s0r[0:1, bass.ds(h * HALF, HALF)])
                        if k == 0:
                            v.load(crows, c0r[0:1, bass.ds(h * HALF, HALF)])
                        for j in range(HALF):
                            bank = SG[(b * HALF + j) % 2]
                            n = i * BODY + (b * HALF + j + T * k)
                            w = v.snap(srows[j], min_val=0, max_val=NSEG - P)
                            e.wait_ge(s["summed"], n + (BODY + 1))
                            e.wait_ge(s["added"], n + 2)
                            v.tensor_tensor(UT[:, bass.ds(w, P)], UT[:, bass.ds(w, P)], bank[:, 0:P], ALU.add).then_inc(s["added"], 1)
                            if k == 0:
                                c = v.snap(crows[j], min_val=0, max_val=(CT - 2) * EW)
                                e.wait_ge(s["e_added"], n + 2)
                                v.tensor_tensor(EC[:, bass.ds(c, 2 * EW)], EC[:, bass.ds(c, 2 * EW)], bank[:, P:P + 2 * EW],
                                                ALU.add).then_inc(s["e_added"], 1)
                    link.end(IT) if False else None
                link.end(IT)

            sums(0)
            e.wait_ge(s["e_added"], 2 + T)
            cnt = ECv[:, :, DE]
            link(v.tensor_scalar(nodec[:, :], ECv[:, :, DE + 1], 256.0, None, ALU.mult))
            link(v.tensor_tensor(nodec[:, :], nodec[:, :], ECv[:, :, DE + 2], ALU.add))
            link(v.tensor_scalar(nodes[:, :], cnt, 0.0, 60000.0, ALU.is_equal, ALU.mult))
            link(v.tensor_tensor(nodes[:, :], nodes[:, :], nodec[:, :], ALU.add))
            link(v.tensor_scalar(nodec[:, :], nodes[:, :], float(N - 1), None, ALU.min))
            link(v.tensor_scalar(inv[:, :], cnt, 1.0, None, ALU.max))
            link(v.reciprocal(inv[:, :], inv[:, :]))
            v.tensor_copy(inv[:, 0:1], inv[:, 0:1]).then_inc(s["ec_ready"], 1) if False else v.sem_inc(s["ec_ready"], 1)
            tw = TABI[:, 0, 0:CT]
            tv = TABI[:, 1, 0:CT]
            link(v.tensor_copy(tw, nodes[:, :]))
            link(v.tensor_scalar(tv, tw, 127, None, ALU.bitwise_and))
            link(v.tensor_copy(nlo[:, :], tv))
            link(v.tensor_scalar(tv, tw, 7, None, ALU.logical_shift_right))
            link(v.tensor_copy(nhi[:, :], tv))
            link(v.tensor_scalar(tv, ti[:, :], 255, None, ALU.bitwise_and))
            link(v.tensor_copy(wlo[:, :], tv))
            link(v.tensor_scalar(tv, ti[:, :], 0x7F00, None, ALU.bitwise_and))
            link(v.tensor_copy(whi[:, :], tv))
            e.wait_ge(s["ld_src"], 16)
            link(v.tensor_scalar(dsti[:, :], srci[:, :], 7, None, ALU.logical_shift_right))
            link(v.tensor_copy(shi[:, 0:T], dsti[:, :]))
            with e.Fori(0, CIT) as i:
                for j in range(2 * CG):
                    c = bass.ds(i * 2 * CG + j, 1)
                    r = j % 2
                    e.wait_ge(s["tab_mm"], i * 2 * CG + (j + 1))
                    v.tensor_scalar(OH[:, r, 0:HI], iotah[:, 0:HI], nhi[:, c], None, ALU.is_equal)
                    v.tensor_scalar(LA[:, r, 0, :], iotah[:, 0:P], nlo[:, c], whi[:, c], ALU.is_equal, ALU.mult)
                    v.tensor_scalar(LA[:, r, 1, :], iotah[:, 0:P], nlo[:, c], wlo[:, c], ALU.is_equal, ALU.mult).then_inc(s["oh_built"], 1)
            e.wait_ge(s["tab_mm"], 2 + CT + 1)
            link(v.tensor_copy(TABI[:, 0, 0:HI], TP[:, 0:HI]))
            link(v.tensor_scalar(TABI[:, 1, 0:HI], TABI[:, 0, 0:HI], 0x7F00, None, ALU.bitwise_and))
            link(v.tensor_copy(TAB[:, 0, 0:HI], TABI[:, 1, 0:HI]))
            link(v.tensor_scalar(TABI[:, 1, 0:HI], TABI[:, 0, 0:HI], 255, None, ALU.bitwise_and))
            link(v.tensor_copy(TAB[:, 1, 0:HI], TABI[:, 1, 0:HI]))
            v.sem_inc(s["tab_ready"], 1)
            with e.Fori(0, IT) as i:
                link.loop(i, 2)
                for b in (0, 1):
                    h = i * 2 + b
                    e.wait_ge(ld_lo[b], i * 16 + 16)
                    link(v.tensor_scalar(SLO[:, b, :], SLO[:, b, :], 127, None, ALU.bitwise_and))
                    e.wait_ge(s["look_mm"], h * HALF + HALF)
                    v.tensor_scalar(OS[:, b, :], SLO[:, b, :], iotap[:, 0:1], None, ALU.is_equal).then_inc(s["os_built"], 1)
                    for j in range(HALF):
                        t = b * HALF + j
                        n = i * BODY + t
                        c = bass.ds(n, 1)
                        e.wait_ge(s["look_mm"], n + (BODY + 1))
                        e.wait_ge(s["looked"], n + 1)
                        v.scalar_tensor_tensor(out=JUNK[:, t % 2, 0:HI], in0=iotah[:, 0:HI], scalar=shi[:, c], in1=LP[t % 2][:, 0:HI],
                                               op0=ALU.is_equal, op1=ALU.mult, accum_out=idx[:, c]).then_inc(s["looked"], 1)
            link.end(IT)

            def stats(e_, src_, b, j, ps):
                v.bn_stats(stat[ps, b, j, :], src_)

            for k in range(4):
                if k:
                    if k == 1:
                        with e.Fori(0, LIT) as i:
                            link.loop(i, 4)
                            for b in (0, 1):
                                g = i * 2 + b
                                e.wait_ge(ld_x[b], i * 16 + 16)
                                for r in range(LR):
                                    last = v.bn_stats(stat[:, b, r, :], XL[:, b, r * D:(r + 1) * D])
                                link(last)
                                v.sem_inc(s["tick"], 1)
                                for r in range(LR):
                                    last = v.bn_aggr(mv[:, b, r, :], stat[:, b, r, :])
                                last.then_inc(s["ln_stat"], 1)
                            for b in (0, 1):
                                g = i * 2 + b
                                e.wait_ge(s["ln_sd"], g + 1)
                                e.wait_ge(s["ln_stat"], g + 1)
                                link(v.reciprocal(rs[:, b, :], sd[:, b, :]))
                                for r in range(LR):
                                    o = XL[:, b, r * D:(r + 1) * D]
                                    last = v.tensor_scalar(o, o, mv[:, b, r, 0:1], rs[:, b, r:r + 1], ALU.subtract, ALU.mult)
                                last.then_inc(s["ln_done"], 1)
                        link.end(LIT)
                        q = slice(0, LREST)
                        e.wait_ge(ld_x[0], 16 * (LIT + 1))
                        link(v.bn_stats(stat[q, 0, 0, :], XL[q, 0, 0:D]))
                        v.bn_aggr(mv[q, 0, 0, :], stat[q, 0, 0, :]).then_inc(s["ln_stat"], 1)
                        e.wait_ge(s["ln_stat"], 2 * LIT + 1)
                        e.wait_ge(s["ln_sd"], 2 * LIT + 1)
                        link(v.reciprocal(rs[q, 0, 0:1], sd[q, 0, 0:1]))
                        v.tensor_scalar(XL[q, 0, 0:D], XL[q, 0, 0:D], mv[q, 0, 0, 0:1], rs[q, 0, 0:1], ALU.subtract, ALU.mult).then_inc(s["ln_done"], 1)
                    e.wait_ge(s["ut_zero"], NG * k)
                    sums(k)
                if k == 3:
                    for b in (0, 1):
                        e.wait_ge(st_h[b], 16 * (CIT * 3 + 1))
                def rows(i, k, peeled=False):
                    for b in (0, 1):
                        g = i * 2 + b
                        iv = inv[:, bass.ds(g * CG, CG)].unsqueeze(2).to_broadcast([P, CG, D])
                        e.wait_ge(s["h_mm"], g + (NG * k + 3))
                        if k < 3:
                            e.wait_ge(st_h[b], i * 16 + 16 * (CIT * k + 1))
                        else:
                            if not peeled:
                                for q in range(CG):
                                    e.wait_ge(scat[b * CG + q], i * 16)
                        v.tensor_tensor(HS[:, b, :].rearrange("p (j c) -> p j c", c=D), HP[b][:, :].rearrange("p (j c) -> p j c", c=D),
                                        iv, ALU.mult).then_inc(s["h_read"], 1)
                        if k < 3:
                            e.wait_ge(s["us_staged"], g + (NG * k + 1))
                            v.tensor_copy(UT[:, bass.ds(g * CW, CW)], ZERO[:, :]).then_inc(s["ut_zero"], 1)
                        else:
                            e.wait_ge(s["h_read"], g + (NG * k + 3))
                            for q in range(CG):
                                e.wait_ge(xg[b * CG + q], i * 16 + 16)
                            xr = G[:, b * CG:(b + 1) * CG, :].rearrange("p j c -> p (j c)")
                            link(v.tensor_tensor(HS[:, b, :], HS[:, b, :], xr, ALU.add))
                            v.sem_inc(s["f_add"], 1)
                            for r in range(CG):
                                last = v.bn_stats(stat[:, b, r, :], HS[:, b, r * D:(r + 1) * D])
                            link(last)
                            v.sem_inc(s["tick"], 1)
                            for r in range(CG):
                                last = v.bn_aggr(mv[:, b, r, :], stat[:, b, r, :])
                            last.then_inc(s["f_stat"], 1)
                    if k == 3:
                        for b in (0, 1):
                            g = i * 2 + b
                            e.wait_ge(s["f_sd"], g + 1)
                            e.wait_ge(s["f_stat"], g + 1)
                            link(v.reciprocal(rs[:, b, 0:CG], sd[:, b, 0:CG]))
                            for r in range(CG):
                                o = HS[:, b, r * D:(r + 1) * D]
                                last = v.tensor_scalar(o, o, mv[:, b, r, 0:1], rs[:, b, r:r + 1], ALU.subtract, ALU.mult)
                            last.then_inc(s["f_out"], 1)
                if k == 3:
                    rows(0, k, True)
                with e.Fori(1 if k == 3 else 0, CIT) as i:
                    if k == 3:
                        link.loop(i - 1, 6)
                    rows(i, k)
                if k == 3:
                    link.end(CIT - 1)

        @block.tensor
        def _(e):
            t = nc.tensor
            for n, c in (("summed", BODY), ("et_mm", 2), ("tab_mm", 2), ("look_mm", BODY), ("h_mm", 2)):
                e.sem_inc(s[n], c)
            e.wait_ge(s["const"], 3)
            e.wait_ge(s["prep_in"], 1)
            t.matmul(LP[0][:, 0:T], tri[:, :], first[:, :], start=True, stop=True)
            t.matmul(LP[1][:, 0:T], ones[:, :], first[:, :], start=True, stop=True)
            t.matmul(HP[0][:, 0:T], row0[:, :], first[:, :], start=True, stop=True).then_inc(s["prep_mm"], 1)

            def sums(k):
                with e.Fori(0, IT) as i:
                    for b in (0, 1):
                        h = i * 2 + b
                        if k == 0:
                            e.wait_ge(s["e_built"], h + 1)
                        for j in range(HALF):
                            slot = b * HALF + j
                            bank = SG[slot % 2]
                            n = i * BODY + (slot + T * k)
                            e.wait_ge(s["s_built"], n + 1)
                            e.wait_ge(s["added"], n + 1)
                            if k == 0:
                                e.wait_ge(s["e_added"], n + 1)
                                for w in (0, 1):
                                    sa = SA[:, j, w * P:(w + 1) * P]
                                    o = bank[:, P + w * EW:P + (w + 1) * EW]
                                    t.matmul(o, sa, EB[:, b, j, 0:EW], start=True, stop=False)
                                    t.matmul(o[:, 0:DE], sa, EB[:, b, j, EW:EW + DE], start=False, stop=False)
                                    t.matmul(o[:, 0:DE], sa, EB[:, b, j, EW + DE:EP], start=False, stop=True)
                            e.wait_ge(gat[slot], i * 16 + (k * IT + 1) * 16)
                            t.matmul(bank[:, 0:P], G[:, slot, :], S[:, j, :], start=True, stop=True).then_inc(s["summed"], 1)

            sums(0)
            with e.Fori(0, CIT) as i:
                for b in (0, 1):
                    g = i * 2 + b
                    e.wait_ge(s["ecs_full"], g + 1)
                    e.wait_ge(s["et_copied"], g + 1)
                    for j in range(CG):
                        last = t.transpose(HP[b][0:DE + 1, j * P:(j + 1) * P], ECS[:, b, j, 0:DE + 1], ident[:, :])
                    last.then_inc(s["et_mm"], 1)
            e.wait_ge(s["added"], 2 + T)
            t.matmul(TP[:, 0:HI], ZH[:, 0:P], ZH[:, 0:HI], start=True, stop=False)
            with e.Fori(0, CIT) as i:
                for j in range(2 * CG):
                    r = j % 2
                    e.wait_ge(s["oh_built"], i * 2 * CG + (j + 1))
                    t.matmul(TP[:, 0:HI], LA[:, r, 0, :], OH[:, r, 0:HI], start=False, stop=False)
                    t.matmul(TP[:, 0:HI], LA[:, r, 1, :], OH[:, r, 0:HI], start=False, stop=False).then_inc(s["tab_mm"], 1)
            t.matmul(TP[:, 0:HI], ZH[:, 0:P], ZH[:, 0:HI], start=False, stop=True).then_inc(s["tab_mm"], 1)
            e.wait_ge(s["tab_ready"], 1)
            with e.Fori(0, IT) as i:
                for b in (0, 1):
                    h = i * 2 + b
                    e.wait_ge(s["os_built"], h + 3)
                    for j in range(HALF):
                        tt = b * HALF + j
                        n = i * BODY + tt
                        e.wait_ge(s["looked"], n + 1)
                        t.matmul(LP[tt % 2][:, 0:HI], OS[:, b, j * P:(j + 1) * P], TAB[:, 0, 0:HI], start=True, stop=False)
                        t.matmul(LP[tt % 2][:, 0:HI], OS[:, b, j * P:(j + 1) * P], TAB[:, 1, 0:HI], start=False, stop=True).then_inc(s["look_mm"], 1)
            e.wait_ge(s["ld_w"], 32)
            e.wait_ge(s["et_copied"], 2 + NG)
            for k in range(4):
                if k:
                    sums(k)
                base = (0, 1, 2, 4)[k]
                with e.Fori(0, CIT) as i:
                    for b in (0, 1):
                        g = i * 2 + b
                        e.wait_ge(s["h_read"], g + (NG * k + 1))
                        e.wait_ge(ld_et[b], i * 16 + 16 * (CIT * k + 1))
                        if k >= 2:
                            e.wait_ge(ld_u1[b], i * 16 + 16 * (CIT * (k - 2) + 1))
                        if k == 3:
                            e.wait_ge(ld_u2[b], i * 16 + 16)
                        e.wait_ge(s["us_staged"], g + (NG * k + 1))
                        ins = [(US, WX[:, base, :])] if k < 2 else [(U1, WX[:, 2, :]), (US, WX[:, 3, :])] if k == 2 else \
                            [(U1, WX[:, 4, :]), (U2, WX[:, 5, :]), (US, WX[:, 6, :])]
                        for j in range(CG):
                            o = HP[b][:, j * P:(j + 1) * P]
                            c = slice(j * P, (j + 1) * P)
                            t.matmul(o, ET[:, b, c], WE[:, k, :], start=True, stop=False)
                            for m, (u, w) in enumerate(ins):
                                last = t.matmul(o, u[:, b, c], w, start=False, stop=m == len(ins) - 1)
                        last.then_inc(s["h_mm"], 1)


def kernel(x, src, dst, edge_attr_16, L0_gnn_W0, L0_gnn_b0, L0_gnn_W1, L0_gnn_b1, L0_gnn_W2, L0_gnn_b2, L0_gnn_W3, L0_gnn_b3):
    import numpy as np
    import concourse.bacc as bacc
    from concourse.bass_utils import run_bass_kernel_spmd

    x, src, dst, ea = (np.asarray(v) for v in (x, src, dst, edge_attr_16))
    Ws = [np.asarray(w) for w in (L0_gnn_W0, L0_gnn_W1, L0_gnn_W2, L0_gnn_W3)]
    bs = [np.asarray(b) for b in (L0_gnn_b0, L0_gnn_b1, L0_gnn_b2, L0_gnn_b3)]
    pad = T * P - E
    dst_p = np.pad(dst, (0, pad), constant_values=HI * P)
    prev_p = np.concatenate([np.full(1, -1, dst.dtype), dst_p[:-1]])
    src_p = np.pad(src, (0, pad))
    cols = lambda a: np.ascontiguousarray(a.reshape(T, P).T)
    ea_p = np.pad(ea, ((0, pad), (0, 0))).reshape(2 * IT, HALF, P, DE).transpose(0, 2, 1, 3)
    wx = np.concatenate([w[:-DE] for w in Ws]).reshape(7, D, D).transpose(1, 0, 2)
    we = np.stack([np.concatenate([w[-DE:], b[None]]) for w, b in zip(Ws, bs)], axis=1)
    arrays = {"x": x, "dst_t": cols(dst_p), "prev_t": cols(prev_p), "src_t": cols(src_p), "src_rows": src_p,
              "ea": ea_p, "wx": wx, "we": we}
    arrays = {k: np.ascontiguousarray(v) for k, v in arrays.items()}
    nc = bacc.Bacc("TRN2", target_bir_lowering=False, num_devices=1)
    args = {k: nc.dram_tensor(k + "_in", v.shape, mybir.dt.from_np(v.dtype), kind="ExternalInput").ap() for k, v in arrays.items()}
    out = nc.dram_tensor("out_rows", (N, D), f32, kind="ExternalOutput").ap()
    gnn_kernel(nc, out=out, **args)
    r = run_bass_kernel_spmd(nc, [{k + "_in": v for k, v in arrays.items()}], core_ids=[0])
    return r.results[0]["out_rows"]
```

```python
import concourse.bass as bass
from concourse import mybir
from concourse.alu_op_type import AluOpType as ALU
from contextlib import ExitStack

P = 128
N, D, E, DE = 50000, 128, 25000, 16
T = (E + P - 1) // P
HALF = 7
BODY = 2 * HALF
IT = T // BODY
CT = 200
CG = 4
CW = CG * P
CIT = CT // (2 * CG)
NSEG = CT * P
WIN = 512
HI = (N + P - 1) // P
EW = DE + 3
EP = 3 * DE + 3
LR = 13
LIT = N // (P * LR * 2) // 3
LREST = N - 3 * LIT * 2 * LR * P
SCH = T * P // 4
EPS = 1e-5
f32, bf16, f16 = mybir.dt.float32, mybir.dt.bfloat16, mybir.dt.float16
i32, u32 = mybir.dt.int32, mybir.dt.uint32
ACT = mybir.ActivationFunctionType
AX = mybir.AxisListType


class Chain:

    def __init__(self, eng, sem):
        self.eng, self.sem, self.base, self.n = eng, sem, 0, 0

    def __call__(self, ins):
        self.n += 1
        ins.then_inc(self.sem, 1)
        self.eng.wait_ge(self.sem, self.base + self.n)

    def begin(self, ins):
        self.n += 1
        ins.then_inc(self.sem, 1)

    def sync(self):
        self.eng.wait_ge(self.sem, self.base + self.n)

    def loop(self, i, per):
        self.start, self.per = self.base + self.n, per
        self.base, self.n = i * per + self.start, 0

    def end(self, count):
        assert self.n == self.per, self.n
        self.base, self.n = count * self.per + self.start, 0


def gnn_kernel(nc, x, dst_t, prev_t, src_t, dst_rows, src_rows, ea, wx, we, out):
    H = [nc.dram_tensor(f"h{k}_rows", [NSEG + 1, D], f32).ap() for k in range(3)]
    UD = [nc.dram_tensor(f"u{k}_cols", [P, NSEG], f32).ap() for k in (1, 2)]
    ETD = nc.dram_tensor("edge_sum_cols", [DE + 1, NSEG], f32).ap()
    XS = nc.dram_tensor("x_of_segments", [NSEG, D], f32).ap()
    SEA = nc.dram_tensor("sorted_features", [T * P, DE], f32).ap()
    SSR = nc.dram_tensor("sorted_src_rows", [T * P, 1], i32).ap()
    SDT, SPT, SST = (nc.dram_tensor(f"sorted_{n}_t", [P * (T + 1), 1], i32).ap() for n in ("dst", "prev", "src"))

    with ExitStack() as ctx:
        sb = lambda n, s, d: ctx.enter_context(nc.sbuf_tensor(n, s, d))
        pb = lambda n: ctx.enter_context(nc.psum_tensor(n, [P, 512], f32))
        sem = lambda n: ctx.enter_context(nc.semaphore(n))

        UT = sb("UT", [P, NSEG], f32)
        ECS_ = sb("EC", [P, CT * EW], f32)
        EC = ECS_[:, :]
        ECv = EC.rearrange("p (c w) -> p c w", w=EW)
        SW = ECS_[:, 0:HALF * WIN].rearrange("p (j w) -> p j w", w=WIN)
        G = sb("G", [P, BODY, D], f32)
        S = sb("S", [P, BODY, P], f32)
        US = sb("US", [P, 2, CW], f32)
        ET = sb("ET", [P, 2, CW], f32)
        HS = sb("HS", [P, 2, CW], f32)
        WX = sb("WX", [P, 7, D], f32)
        WE = sb("WE", [P, 4, D], f32)
        ZERO = sb("ZERO", [P, CW], f32)
        ident = sb("ident", [P, P], f32)
        tri = sb("tri", [P, P], bf16)
        ones = sb("ones", [P, P], bf16)
        row0 = sb("row0", [P, P], bf16)
        iota = sb("iota", [P, WIN], f32)
        iotah = sb("iotah", [P, HI + 1], f16)
        iotap = sb("iotap", [P, 1], f32)
        steps = sb("steps", [P, CIT], f32)
        eps = sb("eps", [P, 1], f32)
        cf = sb("cf", [P, 8], f32)
        counts = sb("counts", [P, 4], i32)
        dsti = sb("dsti", [P, CT], i32)
        previ = sb("previ", [P, CT], i32)
        srci = sb("srci", [P, T + BODY], i32)
        seg = sb("seg", [P, CT], f32)
        rel = sb("rel", [P, CT], f32)
        rela = sb("rela", [P, CT], f32)
        nh = sb("nh", [P, CT], f32)
        nl = sb("nl", [P, CT], f32)
        flag = sb("flag", [P, CT], bf16)
        idx = sb("idx", [P, T + BODY], f32)
        s0r = sb("s0r", [P, CT], i32)
        c0r = sb("c0r", [P, CT], i32)
        V4 = sb("V4", [P, CT, 4], bf16)
        AC = sb("AC", [P, CT * 4], f32)
        ACv = AC[:, :].rearrange("p (c w) -> p c w", w=4)
        ti = sb("ti", [P, CT], i32)
        nodes = sb("nodes", [P, CT], f32)
        nodec = sb("nodec", [P, CT], f32)
        inv = sb("inv", [P, CT], f32)
        nlo, nhi, wlo, whi, shi = (sb(n, [P, CT], f32) for n in ("nlo", "nhi", "wlo", "whi", "shi"))
        istage = sb("istage", [P, 2, HALF], u32)
        nstage = sb("nstage", [P, 2, CG], u32)
        stat = sb("stat", [P, 2, LR, 6], f32)
        mv = sb("mv", [P, 2, LR, 2], f32)
        sd = sb("sd", [P, 2, LR], f32)
        rs = sb("rs", [P, 2, LR], f32)

        AREA = 8480
        area = sb("area", [P, AREA], f32)
        at = [0]

        def carve(shape, dt, size):
            n = 1
            for m in shape:
                n *= m
            words = (n * size + 3) // 4
            ap = area[:, at[0]:at[0] + words]
            at[0] += words
            assert at[0] <= AREA, at[0]
            if dt != f32:
                ap = ap.bitcast(dt)
            names_ = "abc"[:len(shape)]
            if len(shape) > 1:
                ap = ap.rearrange(f"p ({' '.join(names_)}) -> p {' '.join(names_)}", **dict(zip(names_[1:], shape[1:])))
            return ap

        SA = carve([BODY, 2 * P], bf16, 2)
        EF = carve([2, HALF, DE], f32, 4)
        EB = carve([2, HALF, EP + 1], bf16, 2)
        EB_END = at[0]
        ECS = carve([2, CG, EW], f32, 4)
        OH = carve([2, HI + 1], f16, 2)
        LA = carve([2, 2 * P], f16, 2)
        TAB = carve([2, HI + 1], f16, 2)
        TABI = carve([2, HI + 1], i32, 4)
        JUNK = carve([2, HI + 1], f16, 2)
        ZH = ZERO[:, :].bitcast(f16)
        SLO = carve([2, HALF * P], i32, 4)
        OS = carve([2, HALF * P], f16, 2)
        XG = carve([2, CG * D], f32, 4)
        at[0] = 0
        XL = carve([2, LR * D], f32, 4)
        OL = carve([2, LR * D], f32, 4)
        U1 = carve([2, CW], f32, 4)
        U2 = G[:, 0:8, :].rearrange("p (b j) w -> p b (j w)", b=2)
        at[0] = 0
        XR = carve([2, CW], f32, 4)
        at[0] = EB_END
        SJUNK = carve([SCH], bf16, 2)
        SBELOW = carve([P], f32, 4)
        SOWN = carve([P], f32, 4)
        SEF = carve([HALF, DE], f32, 4)
        SACC = carve([T * P // SCH + 2], f32, 4)
        SPOS = carve([3, HALF], u32, 4)
        SPART = carve([4], i32, 4)
        SPAY = carve([2, HALF], i32, 4)
        DB = UT[:, 0:T * P]

        SG = [pb("segp0"), pb("segp1")]
        LP = [pb("lp0"), pb("lp1")]
        TP = pb("tp")
        HP = [pb("hp0"), pb("hp1")]
        LK = LP + HP

        names = ("ld_dst ld_prev ld_src ld_w const dve prep_in prep_mm prep_done zrow tick pool_tick act_tick pe_tick tick_sp "
                 "idx_ready s_built summed accum e_split e_built e_mm e_added ecs_full et_mm et_copied ec_ready "
                 "oh_built tab_mm tab_ready os_built look_mm looked a_built a_mm a_added list_in list_mm list_ready "
                 "ut_clear order_in order_mm order_known ld_bc ld_sort sort_dve rank_ready sorted "
                 "us_staged h_mm h_read ut_zero n_staged sc_staged f_stat f_sd f_out ln_stat ln_sd ln_done").split()
        s = {n: sem(n) for n in names}
        gat = [sem(f"gathered{j}") for j in range(BODY)]
        two = lambda n: [sem(f"{n}{b}") for b in (0, 1)]
        ld_ea, ld_lo, st_et, ld_et, ld_u1, ld_u2, st_u, st_h, ld_x, st_o, st_xs, ld_xr = (
            two(n) for n in "ld_ea ld_lo st_et ld_et ld_u1 ld_u2 st_u st_h ld_x st_o st_xs ld_xr".split())
        scat = [sem(f"scattered{j}") for j in range(2 * CG)]
        xg = [sem(f"x_gathered{j}") for j in range(2 * CG)]
        block = ctx.enter_context(nc.Block())

        view = lambda t: t.rearrange("(g j p) c -> g p j c", p=P, j=CG)
        hrows = [view(h[1:NSEG + 1, :]) for h in H]
        xsrows = view(XS)
        LN_ROWS = 3 * LIT * 2 * LR * P
        xv = x[0:LN_ROWS, :].rearrange("(g p r) c -> g p (r c)", p=P, r=LR)
        ov = out[0:LN_ROWS, :].rearrange("(g p r) c -> g p (r c)", p=P, r=LR)
        one = lambda ap, g: ap[bass.ds(g, 1)]
        rows4 = lambda ap: ap.rearrange("o p j c -> (o p) j c")
        tile4 = lambda ap: ap.rearrange("p (j c) -> p j c", c=D)

        def seg_steps(e):
            e.wait_ge(s["ec_ready"], 1)
            return e.value_load(counts[0:1, 0:1], min_val=1, max_val=CIT)

        def edge_steps(e):
            e.wait_ge(s["list_ready"], 1)
            return e.value_load(counts[0:1, 1:2], min_val=1, max_val=IT)

        SCATTERS = HALF * 5 * 16

        def unsorted(e):
            e.wait_ge(s["order_known"], 1)
            return e.value_load(counts[0:1, 3:4], min_val=0, max_val=T * P)

        @block.sync
        def _(e):
            e.dma_start(dsti[:, 0:T], dst_t).then_inc(s["ld_dst"], 16)
            e.dma_start(previ[:, 0:T], prev_t).then_inc(s["ld_prev"], 16)
            e.dma_start(srci[:, 0:T], src_t).then_inc(s["ld_src"], 16)
            bad = unsorted(e)
            with e.If(bad > 0):
                e.dma_start(DB.bitcast(i32), dst_rows.partition_broadcast(P)).then_inc(s["ld_bc"], 16)
                e.dma_start(SPT[0:1, :], prev_t[0:1, 0:1]).then_inc(s["ld_bc"], 16)
                with e.Fori(0, 2 * IT) as i:
                    e.dma_start(SEF, one(ea, i).rearrange("o p j w -> (o p) j w")).then_inc(s["ld_sort"], 16)
                    e.wait_ge(s["sorted"], i * SCATTERS + SCATTERS)
                    e.sem_inc(s["tick_sp"], 1)
                e.wait_ge(s["ld_bc"], 32)
                for arr, col, n in ((dsti, SDT, "ld_dst"), (previ, SPT, "ld_prev"), (srci, SST, "ld_src")):
                    e.dma_start(arr[:, 0:T], col.rearrange("(p t) o -> p (t o)", p=P)[:, 0:T]).then_inc(s[n], 16)
            with e.If(bad < 1):
                for n in ("ld_dst", "ld_prev", "ld_src"):
                    e.sem_inc(s[n], 16)
            sea = SEA.rearrange("(h j p) w -> h p j w", p=P, j=HALF)
            e.dma_start(WX[:, :, :], wx).then_inc(s["ld_w"], 16)
            e.wait_ge(s["const"], 1)
            e.dma_start(WE[0:DE + 1, :, :], we).then_inc(s["ld_w"], 16)
            for k in range(3):
                e.dma_start(H[k][0:1, :], ZERO[0:1, 0:D]).then_inc(s["zrow"], 16)
            for b in (0, 1):
                e.sem_inc(st_et[b], 16)
                e.sem_inc(st_h[b], 16)
                e.sem_inc(st_o[b], 16)
            with e.Fori(0, IT) as i:
                for b in (0, 1):
                    h = i * 2 + b
                    e.wait_ge(s["e_split"], h + 1)
                    e.sem_inc(s["tick_sp"], 1)
                    with e.If(bad > 0):
                        e.dma_start(EF[:, b, :, :], one(sea, h).rearrange("o p j w -> (o p) j w")).then_inc(ld_ea[b], 16)
                    with e.If(bad < 1):
                        e.dma_start(EF[:, b, :, :], one(ea, h).rearrange("o p j w -> (o p) j w")).then_inc(ld_ea[b], 16)
            n_s = seg_steps(e)
            with e.Fori(0, CIT) as i:
                with e.If(i >= n_s):
                    for k in range(3):
                        for b in (0, 1):
                            e.dma_start(rows4(one(hrows[k], i * 2 + b)), tile4(ZERO[:, :])).then_inc(s["zrow"], 16)
            with e.Fori(0, CIT) as i:
                with e.If(i < n_s):
                    for b in (0, 1):
                        g = i * 2 + b
                        e.wait_ge(s["et_copied"], g + 3)
                        e.dma_start(ETD[:, bass.ds(g * CW, CW)], ET[0:DE + 1, b, :]).then_inc(st_et[b], 16)
            with e.Fori(0, IT) as i:
                for b in (0, 1):
                    h = i * 2 + b
                    e.wait_ge(s["os_built"], h + 1)
                    e.sem_inc(s["tick_sp"], 1)
                    for rows_, is_ in ((src_rows, bad < 1), (SSR.rearrange("e o -> (e o)"), bad > 0)):
                        with e.If(is_):
                            e.dma_start(SLO[:, b, :], rows_[bass.ds(h * HALF * P, HALF * P)].partition_broadcast(P)).then_inc(ld_lo[b], 16)
            for b in (0, 1):
                e.wait_ge(st_et[b], n_s * 16 + 16)
            e.sem_inc(s["tick_sp"], 1)
            for k in range(4):
                if k == 1:
                    n_e = edge_steps(e)
                if k:
                    e.wait_ge(s["looked"], 4 + T)
                    e.wait_ge(s["a_mm"], 2 + 2 * CIT)
                    for b in (0, 1):
                        e.wait_ge(st_xs[b], n_s * 16 + 16)
                    e.sem_inc(s["tick_sp"], 1)
                    with e.Fori(0, LIT) as i:
                        for b in (0, 1):
                            n = i * 2 + ((k - 1) * 2 * LIT + b)
                            e.wait_ge(s["ln_done"], n + 1)
                            e.dma_start(XL[:, b, :], one(xv, n).rearrange("o p w -> (o p) w")).then_inc(ld_x[b], 16)
                        for b in (0, 1):
                            n = i * 2 + ((k - 1) * 2 * LIT + b)
                            e.wait_ge(s["ln_done"], n + 3)
                            e.dma_start(one(ov, n).rearrange("o p w -> (o p) w"), OL[:, b, :]).then_inc(st_o[b], 16)
                    if k == 3:
                        M = 3 * 2 * LIT
                        e.dma_start(XL[0:LREST, 0, 0:D], x[N - LREST:N, :]).then_inc(ld_x[0], 16)
                        e.wait_ge(s["ln_done"], M + 3)
                        e.dma_start(out[N - LREST:N, :], OL[0:LREST, 0, 0:D]).then_inc(st_o[0], 16)
                        e.wait_ge(st_o[0], 16 * (3 * LIT + 2))
                        e.wait_ge(st_o[1], 16 * (3 * LIT + 1))
                if k >= 2:
                    for b in (0, 1):
                        e.wait_ge(st_u[b], n_s * (16 * (k - 1)) + 16)
                if k == 3:
                    e.wait_ge(s["summed"], n_e * (BODY * 3) + (T + BODY))
                e.sem_inc(s["tick_sp"], 1)

                def loads(i, k):
                    for b in (0, 1):
                        g = i * 2 + b
                        m = n_s * (2 * k) + g
                        cols = bass.ds(g * CW, CW)
                        e.wait_ge(s["h_mm"], m + 1)
                        e.dma_start(ET[0:DE + 1, b, :], ETD[:, cols]).then_inc(ld_et[b], 16)
                        if k >= 2:
                            e.dma_start(U1[:, b, :], UD[0][:, cols]).then_inc(ld_u1[b], 16)
                        if k == 3:
                            e.dma_start(U2[:, b, :], UD[1][:, cols]).then_inc(ld_u2[b], 16)
                        yield b
                    if k == 3:
                        for b in (0, 1):
                            g = i * 2 + b
                            e.wait_ge(s["f_stat"], g + 1)
                            e.dma_start(tile4(XR[:, b, :]), rows4(one(xsrows, g))).then_inc(ld_xr[b], 16)

                def store(i, b, k):
                    g = i * 2 + b
                    e.wait_ge(s["h_read"], n_s * (2 * k) + g + 3)
                    e.dma_start(rows4(one(hrows[k], g)), tile4(HS[:, b, :])).then_inc(st_h[b], 16)

                for b in loads(0, k):
                    pass
                with e.Fori(1, CIT) as i:
                    with e.If(i < n_s):
                        for b in loads(i, k):
                            if k < 3:
                                store(i - 1, b, k)
                if k < 3:
                    for b in (0, 1):
                        store(n_s - 1, b, k)

        @block.gpsimd
        def _(e):
            g = nc.gpsimd
            g.memset(ZERO[:, :], 0.0)
            g.memset(WE[:, :, :], 0.0)
            g.memset(ET[:, :, :], 0.0).then_inc(s["const"], 1)
            g.memset(ones[:, :], 1.0)
            g.memset(tri[:, :], 1.0)
            g.memset(row0[:, :], 1.0)
            g.memset(ident[:, :], 0.0)
            g.memset(eps[:, :], EPS)
            g.memset(EB[:, :, :, DE:DE + 1], 1.0)
            g.iota(iota[:, :], [[1, WIN]], base=0, channel_multiplier=0, allow_small_or_imprecise_dtypes=True)
            g.iota(iotah[:, :], [[1, HI + 1]], base=0, channel_multiplier=0, allow_small_or_imprecise_dtypes=True)
            g.iota(steps[:, :], [[2 * CG * P, CIT]], base=0, channel_multiplier=0, allow_small_or_imprecise_dtypes=True)
            g.iota(ti[:, :], [[P, CT]], base=1, channel_multiplier=1)
            g.iota(iotap[:, :], [[0, 1]], base=0, channel_multiplier=1, allow_small_or_imprecise_dtypes=True).then_inc(s["const"], 1)
            e.wait_ge(s["const"], 2)
            g.affine_select(out=tri[:, :], in_=tri[:, :], compare_op=ALU.is_ge, fill=0.0, base=0, pattern=[[1, P]], channel_multiplier=-1)
            g.affine_select(out=row0[:, :], in_=row0[:, :], compare_op=ALU.is_equal, fill=0.0, base=0, pattern=[[0, P]], channel_multiplier=1)
            g.affine_select(out=ident[:, :], in_=ident[:, :], compare_op=ALU.not_equal, fill=1.0, base=0, pattern=[[1, P]], channel_multiplier=-1).then_inc(s["const"], 1)
            last_node = e.snap(e.to_reg(N - 1))
            last_row = e.snap(e.to_reg(NSEG))
            bad = unsorted(e)
            with e.If(bad > 0):
                with e.Fori(0, 2 * IT) as i:
                    e.wait_ge(s["rank_ready"], i + 1)
                    e.wait_ge(s["ld_sort"], i * 16 + 16)
                    e.sem_inc(s["pool_tick"], 1)
                    for j in range(HALF):
                        for dst_, rows_, w in ((SEA, SEF[:, j, :], 0), (SSR, SPAY[:, 1, j:j + 1], 0), (SDT, SPAY[:, 0, j:j + 1], 1),
                                               (SST, SPAY[:, 1, j:j + 1], 1), (SPT, SPAY[:, 0, j:j + 1], 2)):
                            g.indirect_dma_start(dst_, bass.IndirectOffsetOnAxis(ap=SPOS[:, w, j:j + 1], axis=0), rows_, None,
                                                 bounds_check=last_row, oob_is_err=False).then_inc(s["sorted"], 16)

            def unit(b, u, done, table, last):
                e.wait_ge(s["idx_ready"], u + done[0] + 1)
                e.wait_ge(s["summed"], u * HALF + done[1] + HALF)
                e.sem_inc(s["pool_tick"], 1)
                for j in range(HALF):
                    slot = b * HALF + j
                    g.indirect_dma_start(G[:, slot, :], None, table, bass.IndirectOffsetOnAxis(ap=istage[:, b, j:j + 1], axis=0),
                                         bounds_check=last, oob_is_err=False).then_inc(gat[slot], 16)

            def x_rows(lo, hi, n_s):
                with e.Fori(lo, hi) as i:
                    with e.If(i < n_s):
                        for b in (0, 1):
                            e.wait_ge(s["n_staged"], i * 2 + b + 1)
                            e.wait_ge(st_xs[b], i * 16 + 16)
                            e.sem_inc(s["pool_tick"], 1)
                            for j in range(CG):
                                g.indirect_dma_start(XG[:, b, j * D:(j + 1) * D], None, x,
                                                     bass.IndirectOffsetOnAxis(ap=nstage[:, b, j:j + 1], axis=0),
                                                     bounds_check=last_node, oob_is_err=False).then_inc(xg[b * CG + j], 16)

            with e.Fori(0, HALF) as i:
                for b in (0, 1):
                    unit(b, i * 2 + b, (0, 0), x, last_node)
            n_s = seg_steps(e)
            x_rows(0, CIT, n_s)
            with e.Fori(HALF, IT) as i:
                for b in (0, 1):
                    unit(b, i * 2 + b, (0, 0), x, last_node)
            n_e = edge_steps(e)
            n_z = e.value_load(counts[0:1, 2:3], min_val=0, max_val=CIT)
            e.wait_ge(s["zrow"], n_z * 96 + 48)
            for k in range(1, 4):
                for b in (0, 1):
                    e.wait_ge(st_h[b], n_s * (16 * k) + 16)
                e.sem_inc(s["pool_tick"], 1)
                with e.Fori(0, IT) as i:
                    with e.If(i < n_e):
                        for b in (0, 1):
                            unit(b, i * 2 + b, (n_e * (2 * (k - 1)) + 2 * IT, n_e * (BODY * (k - 1)) + T), H[k - 1], last_row)
            for b in (0, 1):
                e.wait_ge(st_o[b], 16 * (3 * LIT + 1 + (b == 0)))
            with e.Fori(0, CIT) as i:
                with e.If(i < n_s):
                    for b in (0, 1):
                        e.wait_ge(s["sc_staged"], i * 2 + b + 1)
                        e.wait_ge(s["f_out"], i * 2 + b + 1)
                        e.sem_inc(s["pool_tick"], 1)
                        for j in range(CG):
                            g.indirect_dma_start(out, bass.IndirectOffsetOnAxis(ap=nstage[:, b, j:j + 1], axis=0),
                                                 HS[:, b, j * D:(j + 1) * D], None,
                                                 bounds_check=last_node, oob_is_err=False).then_inc(scat[b * CG + j], 16)
            for q in range(2 * CG):
                e.wait_ge(scat[q], n_s * 16)
            e.sem_inc(s["pool_tick"], 1)

        @block.scalar
        def _(e):
            a = nc.scalar
            win = [e.alloc_register(f"awin{j}") for j in range(HALF)]

            def stage_indices(b, u, done, arr):
                e.wait_ge(s["summed"], u * HALF + done + HALF)
                a.copy(istage[:, b, :], arr[:, bass.ds(u * HALF, HALF)]).then_inc(s["idx_ready"], 1)

            def accumulate(b, u, done, width):
                a.load(win, s0r[0:1, bass.ds(u * HALF, HALF)])
                for j in range(HALF):
                    bank = SG[(b * HALF + j) % 2]
                    n = u * HALF + done + j
                    w = a.snap(win[j], min_val=0, max_val=NSEG - width)
                    e.wait_ge(s["summed"], n + (BODY + 1))
                    e.wait_ge(s["accum"], n * 2 + 4)
                    first = UT[:, bass.ds(w, 1)]
                    a.activation(first, bank[:, 0:1], ACT.Identity, bias=first).then_inc(s["accum"], 1)
                    a.copy(UT[:, bass.ds(w + 1, width - 1)], bank[:, 1:width]).then_inc(s["accum"], 1)

            e.sem_inc(s["et_copied"], 2)
            e.sem_inc(s["accum"], 4)
            for b in (0, 1):
                e.sem_inc(st_xs[b], 16)
                e.sem_inc(st_u[b], 16)
            e.wait_ge(s["ld_src"], 32)
            for b in (0, 1):
                stage_indices(b, b, 0, srci)
            e.wait_ge(s["prep_done"], 1)
            e.wait_ge(s["ut_clear"], 1)
            with e.Fori(0, HALF) as i:
                for b in (0, 1):
                    accumulate(b, i * 2 + b, 0, P)
                    stage_indices(b, i * 2 + b + 2, 0, srci)
            n_s = seg_steps(e)

            def nodes_in(i, b):
                a.copy(nstage[:, b, :], nodec[:, bass.ds((i * 2 + b) * CG, CG)]).then_inc(s["n_staged"], 1)

            def x_out(i, b):
                for j in range(CG):
                    e.wait_ge(xg[b * CG + j], i * 16 + 16)
                e.dma_start(rows4(one(xsrows, i * 2 + b)), tile4(XG[:, b, :])).then_inc(st_xs[b], 16)

            def edge_rows(i, b):
                g = i * 2 + b
                e.wait_ge(s["et_mm"], g + 1)
                a.copy(ECS[:, b, :, :], ECv[:, bass.ds(g * CG, CG), :]).then_inc(s["ecs_full"], 1)

            def edge_cols(i, b):
                g = i * 2 + b
                e.wait_ge(s["et_mm"], g + 3)
                e.wait_ge(st_et[b], i * 16 + 16)
                a.copy(ET[0:DE + 1, b, :], HP[b][0:DE + 1, :]).then_inc(s["et_copied"], 1)

            for step_ in (nodes_in, edge_rows, edge_cols):
                for b in (0, 1):
                    step_(0, b)
            with e.Fori(1, CIT) as i:
                with e.If(i < n_s):
                    for b in (0, 1):
                        edge_rows(i, b)
                    for b in (0, 1):
                        x_out(i - 1, b)
                        nodes_in(i, b)
                    for b in (0, 1):
                        edge_cols(i, b)
            for b in (0, 1):
                x_out(n_s - 1, b)
            with e.Fori(HALF, IT) as i:
                for b in (0, 1):
                    accumulate(b, i * 2 + b, 0, P)
                    with e.If(i < IT - 1):
                        stage_indices(b, i * 2 + b + 2, 0, srci)

            def stage(i, b, k):
                g = i * 2 + b
                m = n_s * (2 * k) + g
                e.wait_ge(s["h_mm"], m + 1)
                if k in (1, 2):
                    e.wait_ge(st_u[b], n_s * (16 * (k - 1)) + i * 16 + 16)
                a.copy(US[:, b, :], UT[:, bass.ds(g * CW, CW)]).then_inc(s["us_staged"], 1)
                if k in (1, 2):
                    e.wait_ge(s["us_staged"], m + 1)
                    e.dma_start(UD[k - 1][:, bass.ds(g * CW, CW)], US[:, b, :]).then_inc(st_u[b], 16)

            e.wait_ge(s["accum"], 4 + 2 * T)
            with e.Fori(0, CIT) as i:
                with e.If(i < n_s):
                    for b in (0, 1):
                        stage(i, b, 0)
            n_e = edge_steps(e)
            for k in range(1, 4):
                done = n_e * (BODY * (k - 1)) + T
                e.wait_ge(s["summed"], done + BODY)
                e.wait_ge(s["accum"], n_e * (2 * BODY * (k - 1)) + (2 * T + 4))
                for b in (0, 1):
                    stage_indices(b, b, done, idx)

                def units(i, k, ln):
                    for b in (0, 1):
                        with e.If(i < n_e):
                            accumulate(b, i * 2 + b, done, WIN)
                            with e.If(i + 1 < n_e):
                                stage_indices(b, i * 2 + b + 2, done, idx)
                            e.sem_inc(s["act_tick"], 1)
                        if ln:
                            n = i * 2 + ((k - 1) * 2 * LIT + b)
                            e.wait_ge(s["ln_stat"], n + 1)
                            a.activation(sd[:, b, :], mv[:, b, :, 1], ACT.Sqrt, bias=eps[:, 0:1]).then_inc(s["ln_sd"], 1)

                e.wait_ge(s["ut_zero"], n_s * (2 * k))
                with e.Fori(0, LIT) as i:
                    units(i, k, True)
                if k == 3:
                    M = 3 * 2 * LIT
                    e.wait_ge(s["ln_stat"], M + 1)
                    a.activation(sd[0:LREST, 0, 0:1], mv[0:LREST, 0, 0:1, 1], ACT.Sqrt, bias=eps[0:LREST, 0:1]).then_inc(s["ln_sd"], 1)
                with e.Fori(LIT, IT) as i:
                    units(i, k, False)
                e.wait_ge(s["accum"], n_e * (2 * BODY * k) + (2 * T + 4))
                if k == 3:
                    for b in (0, 1):
                        e.wait_ge(st_u[b], n_s * 32 + 16)

                def deviation(i, b):
                    g = i * 2 + b
                    e.wait_ge(s["f_stat"], g + 3)
                    a.copy(nstage[:, b, :], nodes[:, bass.ds(g * CG, CG)]).then_inc(s["sc_staged"], 1)
                    a.activation(sd[:, b, 0:CG], mv[:, b, 0:CG, 1], ACT.Sqrt, bias=eps[:, 0:1]).then_inc(s["f_sd"], 1)

                for b in (0, 1):
                    stage(0, b, k)
                with e.Fori(1, CIT) as i:
                    with e.If(i < n_s):
                        for b in (0, 1):
                            stage(i, b, k)
                            if k == 3:
                                deviation(i - 1, b)
                if k == 3:
                    for b in (0, 1):
                        deviation(n_s - 1, b)

        @block.vector
        def _(e):
            v = nc.vector
            link = Chain(e, s["dve"])
            for n, c in (("e_added", BODY), ("e_split", 2), ("looked", 4), ("h_read", 2), ("os_built", 2), ("f_stat", 2),
                         ("ln_done", 2), ("a_added", 8)):
                e.sem_inc(s[n], c)
            v.memset(EC, 0.0)
            v.memset(AC[:, :], 0.0)
            et = slice(0, T)
            e.wait_ge(s["ld_dst"], 16)
            e.wait_ge(s["ld_prev"], 16)
            link(v.tensor_tensor(flag[:, et], dsti[:, et], previ[:, et], ALU.is_lt))
            e.sem_inc(s["order_in"], 1)
            e.wait_ge(s["order_mm"], 1)
            link(v.reduce_sum(cf[:, 6:7], TP[:, et], AX.X))
            link(v.tensor_copy(counts[:, 3:4], cf[:, 6:7]))
            e.sem_inc(s["order_known"], 1)
            bad = unsorted(e)
            with e.If(bad > 0):
                slink = Chain(e, s["sort_dve"])
                e.wait_ge(s["const"], 2)
                e.wait_ge(s["ld_src"], 16)
                e.wait_ge(s["ld_bc"], 32)
                slink(v.tensor_copy(DB, DB.bitcast(i32)))
                slink(v.tensor_copy(nl[:, et], dsti[:, et]))
                slink(v.tensor_scalar(SBELOW, iota[:, 0:P], iotap[:, 0:1], None, ALU.is_lt))
                with e.Fori(0, 2 * IT) as i:
                    slink.loop(i, 22 * HALF)
                    for j in range(HALF):
                        c = bass.ds(i * HALF + j, 1)
                        d = nl[:, c]
                        own = UT[:, bass.ds((i * HALF + j) * P, P)]
                        for q in range(4):
                            slink(v.tensor_scalar(SJUNK, DB[:, q * SCH:(q + 1) * SCH], d, None, ALU.is_lt, ALU.add, accum_out=SACC[:, q:q + 1]))
                        slink(v.scalar_tensor_tensor(out=SOWN, in0=own, scalar=d, in1=SBELOW, op0=ALU.is_equal, op1=ALU.mult, accum_out=SACC[:, 4:5]))
                        slink(v.tensor_scalar(own, own, -0.5, None, ALU.add))
                        slink(v.reduce_sum(SACC[:, 5:6], SACC[:, 0:5], AX.X))
                        slink(v.tensor_copy(SPOS[:, 0, j:j + 1], SACC[:, 5:6]))
                        slink(v.tensor_copy(SPAY[:, 0, j:j + 1], dsti[:, c]))
                        slink(v.tensor_copy(SPAY[:, 1, j:j + 1], srci[:, c]))
                        for w in (1, 2):
                            slink(v.tensor_scalar(SACC[:, 5:6], SACC[:, 5:6], float(w - 1), None, ALU.add))
                            slink(v.tensor_copy(SPART[:, 0:1], SACC[:, 5:6]))
                            slink(v.tensor_scalar(SPART[:, 1:2], SPART[:, 0:1], 127, None, ALU.bitwise_and))
                            slink(v.tensor_scalar(SPART[:, 2:3], SPART[:, 0:1], 7, None, ALU.logical_shift_right))
                            slink(v.tensor_scalar(SPART[:, 1:2], SPART[:, 1:2], float(T + 1), None, ALU.mult))
                            slink(v.tensor_tensor(SPOS[:, w, j:j + 1], SPART[:, 1:2], SPART[:, 2:3], ALU.add))
                    e.sem_inc(s["rank_ready"], 1)
                    e.wait_ge(s["sorted"], i * SCATTERS + SCATTERS)
                    e.sem_inc(s["tick"], 1)
                slink.end(2 * IT)
                e.sem_inc(s["tick"], 1)
            e.wait_ge(s["ld_dst"], 32)
            e.wait_ge(s["ld_prev"], 32)
            e.sem_inc(s["tick"], 1)
            link(v.memset(UT[:, :], 0.0))
            e.sem_inc(s["ut_clear"], 1)
            e.wait_ge(s["const"], 3)

            def ranks(out, base, before):
                link(v.tensor_copy(base, LP[1][:, 0:T]))
                link(v.tensor_tensor_scan(out, base, base, 0.0, ALU.add, ALU.bypass))
                if before is not None:
                    link(v.tensor_copy(before, out[:, T - 1:T]))
                link(v.tensor_tensor(base, out, base, ALU.subtract))
                link(v.tensor_tensor(out, base, LP[0][:, 0:T], ALU.add))
                link(v.tensor_scalar(out, out, -1.0, None, ALU.add))

            def loop_steps(total, step, at_):
                n = 2 * CG * P
                link(v.tensor_scalar(cf[:, 2:3], total, -0.5, float(n) / step, ALU.add, ALU.mult))
                link(v.tensor_scalar(JUNKF[:, 0:CIT], steps[:, :], cf[:, 2:3], None, ALU.is_lt, ALU.add, accum_out=cf[:, 3:4]))
                link(v.tensor_scalar(cf[:, 3:4], cf[:, 3:4], 1.0, None, ALU.max))
                link(v.tensor_copy(counts[:, at_:at_ + 1], cf[:, 3:4]))

            JUNKF = nlo
            link(v.tensor_tensor(flag[:, et], dsti[:, et], previ[:, et], ALU.not_equal))
            e.sem_inc(s["prep_in"], 1)
            v.tensor_copy(seg[:, et], flag[:, et])
            v.tensor_scalar(s0r[:, et], dsti[:, et], 8, None, ALU.logical_shift_right)
            link(v.tensor_scalar(c0r[:, et], dsti[:, et], 255, None, ALU.bitwise_and))
            v.tensor_tensor(nh[:, et], s0r[:, et], seg[:, et], ALU.mult)
            link(v.tensor_tensor(nl[:, et], c0r[:, et], seg[:, et], ALU.mult))
            e.wait_ge(s["prep_mm"], 1)
            ranks(seg[:, et], rela[:, et], cf[:, 0:1])
            link(v.tensor_tensor(rela[:, et], rela[:, et], HP[0][:, et], ALU.add))
            link(v.tensor_scalar(rela[:, et], rela[:, et], -1.0, None, ALU.add))
            link(v.tensor_copy(s0r[:, et], rela[:, et]))
            link(v.tensor_scalar(c0r[:, et], s0r[:, et], 7, None, ALU.logical_shift_right))
            link(v.tensor_tensor(rel[:, et], seg[:, et], rela[:, et], ALU.subtract))

            def window_places(ranks_, width):
                link(v.tensor_copy(rela[:, et], c0r[:, et]))
                v.tensor_scalar(c0r[:, et], rela[:, et], float(width), None, ALU.mult)
                link(v.tensor_scalar(shi[:, et], rela[:, et], -float(P), None, ALU.mult))
                link(v.tensor_tensor(rela[:, et], ranks_, shi[:, et], ALU.add))

            window_places(seg[:, et], EW)
            loop_steps(cf[:, 0:1], 2 * CG * P, 0)
            link(v.tensor_scalar(counts[:, 2:3], cf[:, 3:4], -1.0, float(CIT), ALU.mult, ALU.add))
            e.sem_inc(s["prep_done"], 1)
            crows = [e.alloc_register(f"ewin{j}") for j in range(HALF)]

            def build_rows(b, u, done):
                wide = done is not None
                ring = HALF if not wide else BODY
                e.wait_ge(s["summed"], u * HALF + (done if wide else 0) + ring)
                for j in range(HALF):
                    c = bass.ds(u * HALF + j, 1)
                    if wide:
                        v.tensor_scalar(SW[:, j, :], iota[:, :], rel[:, c], None, ALU.is_equal).then_inc(s["s_built"], 1)
                    else:
                        v.tensor_scalar(S[:, b * HALF + j, :], iota[:, 0:P], rel[:, c], None, ALU.is_equal).then_inc(s["s_built"], 1)

            def edge_half(q, h, loads, adds):
                b = q % 2
                if adds:
                    v.load(crows, c0r[0:1, bass.ds((h - 2) * HALF, HALF)])
                e.wait_ge(s["e_mm"], h + 1)
                f = EF[:, b, :, :]
                hi_, mid, lo = (EB[:, b, :, w:w + DE] for w in (0, EW, EW + DE))
                v.tensor_copy(EB[:, b, :, DE + 1], nh[:, bass.ds(h * HALF, HALF)])
                v.tensor_copy(EB[:, b, :, DE + 2], nl[:, bass.ds(h * HALF, HALF)])
                for j in range(HALF):
                    v.tensor_scalar(SA[:, b * HALF + j, :], iota[:, 0:2 * P], rela[:, bass.ds(h * HALF + j, 1)], None, ALU.is_equal)
                    if adds:
                        add_in(b, h - 2, j)
                    if j == 1:
                        e.wait_ge(ld_ea[b], loads)
                        link.begin(v.tensor_copy(hi_, f))
                    if j == 3:
                        link.sync()
                        link.begin(v.tensor_tensor(f, f, hi_, ALU.subtract))
                    if j == 5:
                        link.sync()
                        link.begin(v.tensor_copy(mid, f))
                link.sync()
                link(v.tensor_tensor(lo, f, mid, ALU.subtract))
                e.sem_inc(s["e_split"], 1)
                e.sem_inc(s["e_built"], 1)

            def add_in(b, h, j):
                c = v.snap(crows[j], min_val=0, max_val=(CT - 2) * EW)
                e.wait_ge(s["e_added"], h * HALF + (BODY + j))
                win = EC[:, bass.ds(c, 2 * EW)]
                v.tensor_tensor(win, win, LP[b][:, j * 2 * EW:(j + 1) * 2 * EW], ALU.add).then_inc(s["e_added"], 1)

            def e_add(b, h):
                v.load(crows, c0r[0:1, bass.ds(h * HALF, HALF)])
                e.wait_ge(s["e_mm"], h + 3)
                for j in range(HALF):
                    add_in(b, h, j)

            def edge_step(i, first):
                for q in range(4):
                    if q % 2 == 0:
                        build_rows(q // 2, i * 2 + q // 2, None)
                    edge_half(q, i * 4 + q, i * 32 + (q // 2) * 16 + 16, q > 1 or not first)

            edge_step(0, True)
            with e.Fori(1, HALF) as i:
                link.loop(i - 1, 16)
                edge_step(i, False)
            link.end(HALF - 1)
            for b in (0, 1):
                e_add(b, 2 * IT - 2 + b)

            e.wait_ge(s["e_added"], BODY + T)
            cnt = ECv[:, :, DE]
            link(v.tensor_scalar(nodec[:, :], ECv[:, :, DE + 1], 256.0, None, ALU.mult))
            link(v.tensor_tensor(nodec[:, :], nodec[:, :], ECv[:, :, DE + 2], ALU.add))
            link(v.tensor_scalar(nodes[:, :], cnt, 0.0, 60000.0, ALU.is_equal, ALU.mult))
            link(v.tensor_tensor(nodes[:, :], nodes[:, :], nodec[:, :], ALU.add))
            link(v.tensor_scalar(nodec[:, :], nodes[:, :], float(N - 1), None, ALU.min))
            link(v.tensor_scalar(inv[:, :], cnt, 1.0, None, ALU.max))
            link(v.reciprocal(inv[:, :], inv[:, :]))
            e.sem_inc(s["ec_ready"], 1)
            n_s = seg_steps(e)
            tw, tv = TABI[:, 0, 0:CT], TABI[:, 1, 0:CT]
            link(v.tensor_copy(tw, nodes[:, :]))
            link(v.tensor_scalar(tv, tw, 127, None, ALU.bitwise_and))
            link(v.tensor_copy(nlo[:, :], tv))
            link(v.tensor_scalar(tv, tw, 7, None, ALU.logical_shift_right))
            link(v.tensor_copy(nhi[:, :], tv))
            link(v.tensor_scalar(tv, ti[:, :], 255, None, ALU.bitwise_and))
            link(v.tensor_copy(wlo[:, :], tv))
            link(v.tensor_scalar(tv, ti[:, :], 0x7F00, None, ALU.bitwise_and))
            link(v.tensor_copy(whi[:, :], tv))
            e.wait_ge(s["ld_src"], 32)
            link(v.tensor_scalar(dsti[:, et], srci[:, et], 7, None, ALU.logical_shift_right))
            link(v.tensor_copy(shi[:, et], dsti[:, et]))
            with e.Fori(0, CIT) as i:
                with e.If(i < n_s):
                    for j in range(2 * CG):
                        c = bass.ds(i * 2 * CG + j, 1)
                        r = j % 2
                        e.wait_ge(s["tab_mm"], i * 2 * CG + (j + 1))
                        v.tensor_scalar(OH[:, r, 0:HI], iotah[:, 0:HI], nhi[:, c], None, ALU.is_equal)
                        v.tensor_scalar(LA[:, r, 0:P], iotah[:, 0:P], nlo[:, c], whi[:, c], ALU.is_equal, ALU.mult)
                        v.tensor_scalar(LA[:, r, P:2 * P], iotah[:, 0:P], nlo[:, c], wlo[:, c], ALU.is_equal, ALU.mult).then_inc(s["oh_built"], 1)
            e.wait_ge(s["tab_mm"], n_s * (2 * CG) + 3)
            link(v.tensor_copy(TABI[:, 0, 0:HI], TP[:, 0:HI]))
            link(v.tensor_scalar(TABI[:, 1, 0:HI], TABI[:, 0, 0:HI], 0x7F00, None, ALU.bitwise_and))
            link(v.tensor_copy(TAB[:, 0, 0:HI], TABI[:, 1, 0:HI]))
            link(v.tensor_scalar(TABI[:, 1, 0:HI], TABI[:, 0, 0:HI], 255, None, ALU.bitwise_and))
            link(v.tensor_copy(TAB[:, 1, 0:HI], TABI[:, 1, 0:HI]))
            e.sem_inc(s["tab_ready"], 1)

            def one_hot_src(i, q, h):
                b = q % 2
                e.wait_ge(ld_lo[b], i * 32 + (q // 2) * 16 + 16)
                link(v.tensor_scalar(SLO[:, b, :], SLO[:, b, :], 127, None, ALU.bitwise_and))
                e.wait_ge(s["look_mm"], h * HALF + HALF)
                v.tensor_scalar(OS[:, b, :], SLO[:, b, :], iotap[:, 0:1], None, ALU.is_equal).then_inc(s["os_built"], 1)

            def select(q, h):
                for j in range(HALF):
                    t = (q * HALF + j) % 2
                    c = bass.ds(h * HALF + j, 1)
                    e.wait_ge(s["look_mm"], h * HALF + (BODY + 1 + j))
                    e.wait_ge(s["looked"], h * HALF + (j + 3))
                    v.scalar_tensor_tensor(out=JUNK[:, t, 0:HI], in0=iotah[:, 0:HI], scalar=shi[:, c], in1=LK[(q * HALF + j) % 4][:, 0:HI],
                                           op0=ALU.is_equal, op1=ALU.mult, accum_out=idx[:, c]).then_inc(s["looked"], 1)

            with e.Fori(0, HALF) as i:
                link.loop(i, 4)
                for q in range(4):
                    if q % 2 == 0:
                        build_rows(q // 2, i * 2 + (2 * HALF + q // 2), None)
                    one_hot_src(i, q, i * 4 + q)
                    if q:
                        select(q - 1, i * 4 + (q - 1))
                select(3, i * 4 + 3)
            link.end(HALF)

            e.wait_ge(s["looked"], 4 + T)
            v.memset(idx[:, T:CT], 0.0)
            v.memset(seg[:, T:CT], 0.0)
            v.memset(rela[:, T:CT], -1.0)
            link(v.memset(c0r[:, T:CT], 0))
            link(v.tensor_scalar(flag[:, et], idx[:, et], 0.0, None, ALU.is_gt))
            e.sem_inc(s["list_in"], 1)
            for w, arr in ((0, idx), (2, seg)):
                link(v.tensor_copy(dsti[:, :], arr[:, 0:CT]))
                link(v.tensor_scalar(previ[:, :], dsti[:, :], 8, None, ALU.logical_shift_right))
                link(v.tensor_copy(V4[:, :, w], previ[:, :]))
                link(v.tensor_scalar(previ[:, :], dsti[:, :], 255, None, ALU.bitwise_and))
                link(v.tensor_copy(V4[:, :, w + 1], previ[:, :]))
            e.wait_ge(s["list_mm"], 1)
            ranks(wlo[:, et], whi[:, et], cf[:, 1:2])
            link(v.tensor_copy(dsti[:, et], whi[:, et]))
            link(v.tensor_scalar(c0r[:, et], dsti[:, et], 7, None, ALU.logical_shift_right))
            window_places(wlo[:, et], 4)
            link(v.tensor_scalar(rela[:, et], rela[:, et], 1.0, None, ALU.add))
            link(v.tensor_tensor(rela[:, et], rela[:, et], flag[:, et], ALU.mult))
            link(v.tensor_scalar(rela[:, et], rela[:, et], -1.0, None, ALU.add))

            def group_rows(i, k):
                for b in (0, 1):
                    g = i * 2 + b
                    iv = inv[:, bass.ds(g * CG, CG)].unsqueeze(2).to_broadcast([P, CG, D])
                    e.wait_ge(s["h_mm"], g + n_s * (2 * k) + 3)
                    e.wait_ge(st_h[b], n_s * (16 * k) + (i * 16 + 16))
                    v.tensor_tensor(tile4(HS[:, b, :]), tile4(HP[b][:, :]), iv, ALU.mult).then_inc(s["h_read"], 1)
                    e.wait_ge(s["us_staged"], g + n_s * (2 * k) + 1)
                    v.tensor_copy(UT[:, bass.ds(g * CW, CW)], ZERO[:, :]).then_inc(s["ut_zero"], 1)

            arow = crows[0:4]
            def list_build(i):
                for q in (0, 1):
                    e.wait_ge(s["a_mm"], i * 2 + (q + 1))
                    for j in range(4):
                        v_ = v.tensor_scalar(SA[:, q * 4 + j, :], iota[:, 0:2 * P], rela[:, bass.ds(i * 8 + (q * 4 + j), 1)], None, ALU.is_equal)
                    v_.then_inc(s["a_built"], 1)

            def list_add(i):
                for q in (0, 1):
                    v.load(arow, c0r[0:1, bass.ds(i * 8 + q * 4, 4)])
                    e.wait_ge(s["a_mm"], i * 2 + (q + 3))
                    for j in range(4):
                        c = v.snap(arow[j], min_val=0, max_val=(CT - 2) * 4)
                        e.wait_ge(s["a_added"], i * 8 + (8 + q * 4 + j))
                        w = AC[:, bass.ds(c, 8)]
                        v.tensor_tensor(w, w, LP[q][:, j * 8:(j + 1) * 8], ALU.add).then_inc(s["a_added"], 1)

            list_build(0)
            list_add(0)
            with e.Fori(1, CIT) as i:
                list_build(i)
                with e.If(i <= n_s):
                    group_rows(i - 1, 0)
                list_add(i)
            with e.If(n_s > CIT - 1):
                group_rows(CIT - 1, 0)
            e.wait_ge(s["a_added"], 8 + CT)
            link(v.tensor_copy(V4[:, :, :], ACv))
            e.sem_inc(s["list_in"], 1)
            for w, arr in ((0, nlo), (2, nhi)):
                link(v.tensor_scalar(arr[:, :], ACv[:, :, w], 256.0, None, ALU.mult))
                link(v.tensor_tensor(arr[:, :], arr[:, :], ACv[:, :, w + 1], ALU.add))
            e.wait_ge(s["list_mm"], 2)
            link(v.tensor_scalar(wlo[:, :], LP[0][:, 0:CT], 256.0, None, ALU.mult))
            link(v.tensor_tensor(wlo[:, :], wlo[:, :], LP[1][:, 0:CT], ALU.add))
            link(v.tensor_tensor(whi[:, :], nhi[:, :], wlo[:, :], ALU.subtract))
            link(v.tensor_copy(shi[:, :], ti[:, :]))
            link(v.tensor_scalar(shi[:, :], shi[:, :], iotap[:, 0:1], cf[:, 1:2], ALU.subtract, ALU.is_gt))
            link(v.tensor_scalar(shi[:, :], shi[:, :], float(NSEG - WIN), None, ALU.mult))
            link(v.tensor_tensor(wlo[:, :], wlo[:, :], shi[:, :], ALU.add))
            link(v.tensor_scalar(flag[:, :], whi[:, :], float(WIN - 1), None, ALU.is_gt))
            e.sem_inc(s["list_in"], 1)
            e.wait_ge(s["list_mm"], 3)
            link(v.reduce_max(cf[:, 4:5], TP[:, 0:CT], AX.X))
            link(v.tensor_scalar(cf[:, 4:5], cf[:, 4:5], 0.0, None, ALU.is_gt))
            link(v.tensor_copy(shi[:, et], s0r[:, et]))
            for all_, listed in ((idx, nlo), (rel, whi), (shi, wlo), (cf, None)):
                a_, l_ = (all_[:, et], listed[:, et]) if listed is not None else (cf[:, 5:6], cf[:, 1:2])
                if listed is None:
                    link(v.memset(cf[:, 5:6], float(T * P)))
                link(v.tensor_tensor(a_, a_, l_, ALU.subtract))
                link(v.scalar_tensor_tensor(out=a_, in0=a_, scalar=cf[:, 4:5], in1=l_, op0=ALU.mult, op1=ALU.add))
            link(v.tensor_copy(s0r[:, et], shi[:, et]))
            loop_steps(cf[:, 5:6], BODY * P, 1)
            e.sem_inc(s["list_ready"], 1)
            n_e = edge_steps(e)

            def norm_stats(b, rows, cols, src_):
                for r in range(rows):
                    last = v.bn_stats(stat[cols, b, r, :], src_[cols, b, r * D:(r + 1) * D])
                link(last)
                e.sem_inc(s["tick"], 1)
                for r in range(rows):
                    last = v.bn_aggr(mv[cols, b, r, :], stat[cols, b, r, :])
                return last

            def norm_rows(b, rows, cols, src_, dst_):
                link(v.reciprocal(rs[cols, b, 0:rows], sd[cols, b, 0:rows]))
                for r in range(rows):
                    c = slice(r * D, (r + 1) * D)
                    last = v.tensor_scalar(dst_[cols, b, c], src_[cols, b, c], mv[cols, b, r, 0:1], rs[cols, b, r:r + 1], ALU.subtract, ALU.mult)
                return last

            al = slice(0, P)
            for k in range(1, 4):
                done = n_e * (BODY * (k - 1)) + T
                with e.Fori(0, LIT) as i:
                    link.loop(i, 4)
                    for b in (0, 1):
                        n = i * 2 + ((k - 1) * 2 * LIT + b)
                        with e.If(i < n_e):
                            build_rows(b, i * 2 + b, done)
                        e.wait_ge(ld_x[b], i * 16 + ((k - 1) * LIT + 1) * 16)
                        norm_stats(b, LR, al, XL).then_inc(s["ln_stat"], 1)
                    for b in (0, 1):
                        n = i * 2 + ((k - 1) * 2 * LIT + b)
                        e.wait_ge(s["ln_stat"], n + 1)
                        e.wait_ge(s["ln_sd"], n + 1)
                        e.wait_ge(st_o[b], i * 16 + ((k - 1) * LIT + 1) * 16)
                        norm_rows(b, LR, al, XL, OL).then_inc(s["ln_done"], 1)
                link.end(LIT)
                if k == 3:
                    M = 3 * 2 * LIT
                    q = slice(0, LREST)
                    e.wait_ge(ld_x[0], 16 * (3 * LIT + 1))
                    norm_stats(0, 1, q, XL).then_inc(s["ln_stat"], 1)
                    e.wait_ge(s["ln_stat"], M + 1)
                    e.wait_ge(s["ln_sd"], M + 1)
                    e.wait_ge(st_o[0], 16 * (3 * LIT + 1))
                    norm_rows(0, 1, q, XL, OL).then_inc(s["ln_done"], 1)
                with e.Fori(LIT, IT) as i:
                    with e.If(i < n_e):
                        for b in (0, 1):
                            build_rows(b, i * 2 + b, done)
                if k < 3:
                    with e.Fori(0, CIT) as i:
                        with e.If(i < n_s):
                            group_rows(i, k)
            for b in (0, 1):
                e.wait_ge(st_h[b], n_s * 48 + 16)

            def last_rows(i, peeled):
                for b in (0, 1):
                    g = i * 2 + b
                    iv = inv[:, bass.ds(g * CG, CG)].unsqueeze(2).to_broadcast([P, CG, D])
                    e.wait_ge(s["h_mm"], g + n_s * 6 + 3)
                    if not peeled:
                        for q in range(CG):
                            e.wait_ge(scat[b * CG + q], i * 16)
                    v.tensor_tensor(tile4(HS[:, b, :]), tile4(HP[b][:, :]), iv, ALU.mult).then_inc(s["h_read"], 1)
                    e.wait_ge(s["h_read"], g + n_s * 6 + 3)
                    e.wait_ge(ld_xr[b], i * 16 + 16)
                    link(v.tensor_tensor(HS[:, b, :], HS[:, b, :], XR[:, b, :], ALU.add))
                    norm_stats(b, CG, al, HS).then_inc(s["f_stat"], 1)
                for b in (0, 1):
                    g = i * 2 + b
                    e.wait_ge(s["f_stat"], g + 3)
                    e.wait_ge(s["f_sd"], g + 1)
                    norm_rows(b, CG, al, HS, HS).then_inc(s["f_out"], 1)

            last_rows(0, True)
            with e.Fori(1, CIT) as i:
                link.loop(i - 1, 6)
                with e.If(i < n_s):
                    last_rows(i, False)

        @block.tensor
        def _(e):
            t = nc.tensor
            for n, c in (("summed", BODY), ("e_mm", 2), ("et_mm", 2), ("tab_mm", 2), ("look_mm", BODY), ("a_mm", 2), ("h_mm", 2)):
                e.sem_inc(s[n], c)
            e.wait_ge(s["const"], 3)
            e.wait_ge(s["order_in"], 1)
            t.matmul(TP[:, 0:T], ones[:, :], flag[:, 0:T], start=True, stop=True).then_inc(s["order_mm"], 1)
            e.wait_ge(s["prep_in"], 1)
            t.matmul(LP[0][:, 0:T], tri[:, :], flag[:, 0:T], start=True, stop=True)
            t.matmul(LP[1][:, 0:T], ones[:, :], flag[:, 0:T], start=True, stop=True)
            t.matmul(HP[0][:, 0:T], row0[:, :], flag[:, 0:T], start=True, stop=True).then_inc(s["prep_mm"], 1)
            e.wait_ge(s["prep_done"], 1)

            def sum_tile(b, u, j, done, step):
                slot = b * HALF + j
                bank = SG[slot % 2]
                n = u * HALF + (0 if done is None else done) + j
                e.wait_ge(s["s_built"], n + 1)
                e.wait_ge(s["accum"], n * 2 + 2)
                e.wait_ge(gat[slot], step * 16)
                rhs, width = (S[:, slot, :], P) if done is None else (SW[:, j, :], WIN)
                t.matmul(bank[:, 0:width], G[:, slot, :], rhs, start=True, stop=True).then_inc(s["summed"], 1)

            def sums(b, u, done, step):
                for j in range(HALF):
                    sum_tile(b, u, j, done, step)

            def with_sums(q, j, i):
                b = q // 2
                if q % 2 == j % 2:
                    sum_tile(b, i * 2 + b, j // 2 + (0 if q % 2 == 0 else 4), None, i + 1)

            def edge_sums(i, q, h):
                b = q % 2
                e.wait_ge(s["e_built"], h + 1)
                e.wait_ge(s["e_added"], h * HALF + HALF)
                for j in range(HALF):
                    for w in (0, 1):
                        sa = SA[:, b * HALF + j, w * P:(w + 1) * P]
                        o = LP[b][:, (2 * j + w) * EW:(2 * j + w + 1) * EW]
                        t.matmul(o, sa, EB[:, b, j, 0:EW], start=True, stop=False)
                        t.matmul(o[:, 0:DE], sa, EB[:, b, j, EW:EW + DE], start=False, stop=False)
                        last = t.matmul(o[:, 0:DE], sa, EB[:, b, j, EW + DE:EP], start=False, stop=True)
                    if j == HALF - 1:
                        last.then_inc(s["e_mm"], 1)
                    with_sums(q, j, i)

            with e.Fori(0, HALF) as i:
                for q in range(4):
                    edge_sums(i, q, i * 4 + q)
            n_s = seg_steps(e)
            t.matmul(TP[:, 0:HI], ZH[:, 0:P], ZH[:, 0:HI], start=True, stop=False)
            with e.Fori(0, CIT) as i:
                with e.If(i < n_s):
                    for j in range(2 * CG):
                        r = j % 2
                        e.wait_ge(s["oh_built"], i * 2 * CG + (j + 1))
                        t.matmul(TP[:, 0:HI], LA[:, r, 0:P], OH[:, r, 0:HI], start=False, stop=False)
                        t.matmul(TP[:, 0:HI], LA[:, r, P:2 * P], OH[:, r, 0:HI], start=False, stop=False).then_inc(s["tab_mm"], 1)
                    for b in (0, 1):
                        g = i * 2 + b
                        e.wait_ge(s["ecs_full"], g + 1)
                        e.wait_ge(s["et_copied"], g + 1)
                        for j in range(CG):
                            last = t.transpose(HP[b][0:DE + 1, j * P:(j + 1) * P], ECS[:, b, j, 0:DE + 1], ident[:, :])
                        last.then_inc(s["et_mm"], 1)
            t.matmul(TP[:, 0:HI], ZH[:, 0:P], ZH[:, 0:HI], start=False, stop=True).then_inc(s["tab_mm"], 1)
            e.wait_ge(s["tab_ready"], 1)

            e.wait_ge(s["et_copied"], n_s * 2 + 2)
            e.sem_inc(s["pe_tick"], 1)

            def look_up(i, q, h):
                e.wait_ge(s["os_built"], h + 3)
                for j in range(HALF):
                    bank = LK[(q * HALF + j) % 4]
                    e.wait_ge(s["looked"], h * HALF + (j + 1))
                    w = OS[:, q % 2, j * P:(j + 1) * P]
                    t.matmul(bank[:, 0:HI], w, TAB[:, 0, 0:HI], start=True, stop=False)
                    t.matmul(bank[:, 0:HI], w, TAB[:, 1, 0:HI], start=False, stop=True).then_inc(s["look_mm"], 1)
                    with_sums(q, j, i + HALF)

            with e.Fori(0, HALF) as i:
                for q in range(4):
                    look_up(i, q, i * 4 + q)
            e.wait_ge(s["looked"], 4 + T)
            e.wait_ge(s["list_in"], 1)
            t.matmul(LP[0][:, 0:T], tri[:, :], flag[:, 0:T], start=True, stop=True)
            t.matmul(LP[1][:, 0:T], ones[:, :], flag[:, 0:T], start=True, stop=True).then_inc(s["list_mm"], 1)
            e.wait_ge(s["ld_w"], 32)
            e.wait_ge(s["et_copied"], n_s * 2 + 2)
            e.sem_inc(s["pe_tick"], 1)

            def products(i, k):
                base = (0, 1, 2, 4)[k]
                for b in (0, 1):
                    g = i * 2 + b
                    m = g + n_s * (2 * k)
                    e.wait_ge(s["h_read"], m + 1)
                    e.wait_ge(ld_et[b], n_s * (16 * k) + (i * 16 + 16))
                    if k >= 2:
                        e.wait_ge(ld_u1[b], n_s * (16 * (k - 2)) + (i * 16 + 16))
                    if k == 3:
                        e.wait_ge(ld_u2[b], i * 16 + 16)
                    e.wait_ge(s["us_staged"], m + 1)
                    ins = [(US, WX[:, base, :])] if k < 2 else [(U1, WX[:, 2, :]), (US, WX[:, 3, :])] if k == 2 else \
                        [(U1, WX[:, 4, :]), (U2, WX[:, 5, :]), (US, WX[:, 6, :])]
                    for j in range(CG):
                        o = HP[b][:, j * P:(j + 1) * P]
                        c = slice(j * P, (j + 1) * P)
                        t.matmul(o, ET[:, b, c], WE[:, k, :], start=True, stop=False)
                        for m_, (u, w) in enumerate(ins):
                            last = t.matmul(o, u[:, b, c], w, start=False, stop=m_ == len(ins) - 1)
                    last.then_inc(s["h_mm"], 1)

            with e.Fori(0, CIT) as i:
                for q in (0, 1):
                    e.wait_ge(s["a_built"], i * 2 + (q + 1))
                    e.wait_ge(s["a_added"], i * 8 + (4 * q + 4))
                    for j in range(4):
                        for w in (0, 1):
                            last = t.matmul(LP[q][:, j * 8 + w * 4:j * 8 + w * 4 + 4], SA[:, q * 4 + j, w * P:(w + 1) * P],
                                            V4[:, bass.ds(i * 8 + (q * 4 + j), 1), :].rearrange("p o c -> p (o c)"), start=True, stop=True)
                    last.then_inc(s["a_mm"], 1)
                with e.If(i < n_s):
                    products(i, 0)
            e.wait_ge(s["list_in"], 2)
            t.matmul(LP[0][:, 0:CT], row0[:, :], V4[:, :, 2], start=True, stop=True)
            t.matmul(LP[1][:, 0:CT], row0[:, :], V4[:, :, 3], start=True, stop=True).then_inc(s["list_mm"], 1)
            e.wait_ge(s["list_in"], 3)
            t.matmul(TP[:, 0:CT], ones[:, :], flag[:, :], start=True, stop=True).then_inc(s["list_mm"], 1)
            n_e = edge_steps(e)
            for k in range(1, 4):
                with e.Fori(0, IT) as i:
                    with e.If(i < n_e):
                        for b in (0, 1):
                            sums(b, i * 2 + b, n_e * (BODY * (k - 1)) + T, n_e * (k - 1) + (i + IT + 1))
                with e.Fori(0, CIT) as i:
                    with e.If(i < n_s):
                        products(i, k)


def kernel(x, src, dst, edge_attr_16, L0_gnn_W0, L0_gnn_b0, L0_gnn_W1, L0_gnn_b1, L0_gnn_W2, L0_gnn_b2, L0_gnn_W3, L0_gnn_b3):
    import numpy as np
    import concourse.bacc as bacc
    from concourse.bass_utils import run_bass_kernel_spmd

    x, src, dst, ea = (np.asarray(v) for v in (x, src, dst, edge_attr_16))
    Ws = [np.asarray(w) for w in (L0_gnn_W0, L0_gnn_W1, L0_gnn_W2, L0_gnn_W3)]
    bs = [np.asarray(b) for b in (L0_gnn_b0, L0_gnn_b1, L0_gnn_b2, L0_gnn_b3)]
    pad = T * P - E
    dst_p = np.pad(dst, (0, pad), constant_values=HI * P)
    prev_p = np.concatenate([np.full(1, -1, dst.dtype), dst_p[:-1]])
    src_p = np.pad(src, (0, pad))
    cols = lambda a: np.ascontiguousarray(a.reshape(T, P).T)
    ea_p = np.pad(ea, ((0, pad), (0, 0))).reshape(2 * IT, HALF, P, DE).transpose(0, 2, 1, 3)
    wx = np.concatenate([w[:-DE] for w in Ws]).reshape(7, D, D).transpose(1, 0, 2)
    we = np.stack([np.concatenate([w[-DE:], b[None]]) for w, b in zip(Ws, bs)], axis=1)
    arrays = {"x": x, "dst_t": cols(dst_p), "prev_t": cols(prev_p), "src_t": cols(src_p), "dst_rows": dst_p, "src_rows": src_p,
              "ea": ea_p, "wx": wx, "we": we}
    arrays = {k: np.ascontiguousarray(v) for k, v in arrays.items()}
    nc = bacc.Bacc("TRN2", target_bir_lowering=False, num_devices=1)
    args = {k: nc.dram_tensor(k + "_in", v.shape, mybir.dt.from_np(v.dtype), kind="ExternalInput").ap() for k, v in arrays.items()}
    out = nc.dram_tensor("out_rows", (N, D), f32, kind="ExternalOutput").ap()
    gnn_kernel(nc, out=out, **args)
    r = run_bass_kernel_spmd(nc, [{k + "_in": v for k, v in arrays.items()}], core_ids=[0])
    return r.results[0]["out_rows"]
```

```python
import concourse.bass as bass
from concourse import mybir
from concourse.alu_op_type import AluOpType as ALU
from contextlib import ExitStack

P = 128
N, D, E, DE = 50000, 128, 25000, 16
T = (E + P - 1) // P
HALF = 7
BODY = 2 * HALF
IT = T // BODY
CT = 200
CG = 4
CW = CG * P
CIT = CT // (2 * CG)
NSEG = CT * P
WIN = 512
HI = (N + P - 1) // P
EW = DE + 3
EP = 3 * DE + 3
BLOCKS = ((0, 0), (0, 1), (0, 2), (1, 0), (1, 1), (2, 0))
EK = DE + 1
ES = len(BLOCKS) * EK
XT = 2
LR = 13
PARTS = ((0, 7), (7, LR))
AR = 2
LIT = N // (P * LR * 2) // 3
LREST = N - 3 * LIT * 2 * LR * P
SCH = T * P // 4
EARLY = 8
EPS = 1e-5
f32, bf16, f16 = mybir.dt.float32, mybir.dt.bfloat16, mybir.dt.float16
i32, u32 = mybir.dt.int32, mybir.dt.uint32
ACT = mybir.ActivationFunctionType
AX = mybir.AxisListType


class Chain:

    def __init__(self, eng, sem):
        self.eng, self.sem, self.base, self.n = eng, sem, 0, 0

    def __call__(self, ins):
        self.n += 1
        ins.then_inc(self.sem, 1)
        self.eng.wait_ge(self.sem, self.base + self.n)

    def begin(self, ins):
        self.n += 1
        ins.then_inc(self.sem, 1)

    def sync(self):
        self.eng.wait_ge(self.sem, self.base + self.n)

    def loop(self, i, per):
        self.start, self.per = self.base + self.n, per
        self.base, self.n = i * per + self.start, 0

    def end(self, count):
        assert self.n == self.per, self.n
        self.base, self.n = count * self.per + self.start, 0


def gnn_kernel(nc, x, dst_t, prev_t, src_t, dst_rows, src_rows, ea, wx, we, part_of_block, out):
    H = nc.dram_tensor("h_rows", [NSEG + 1, D], f32).ap()
    UD = [nc.dram_tensor(f"u{k}_cols", [P, NSEG], f32).ap() for k in (1, 2)]
    ETD = nc.dram_tensor("edge_sum_cols", [ES, NSEG], bf16).ap()
    XS = nc.dram_tensor("x_of_segments", [NSEG, D], f32).ap()
    SEA = nc.dram_tensor("sorted_features", [T * P, DE], f32).ap()
    SSR = nc.dram_tensor("sorted_src_rows", [T * P, 1], i32).ap()
    SDT, SPT, SST = (nc.dram_tensor(f"sorted_{n}_t", [P * (T + 1), 1], i32).ap() for n in ("dst", "prev", "src"))

    with ExitStack() as ctx:
        sb = lambda n, s, d: ctx.enter_context(nc.sbuf_tensor(n, s, d))
        pb = lambda n: ctx.enter_context(nc.psum_tensor(n, [P, 512], f32))
        sem = lambda n: ctx.enter_context(nc.semaphore(n))

        UT = sb("UT", [P, NSEG], f32)
        ECS_ = sb("EC", [P, CT * EW], f32)
        EC = ECS_[:, :]
        ECv = EC.rearrange("p (c w) -> p c w", w=EW)
        SW = ECS_[:, 0:HALF * WIN].rearrange("p (j w) -> p j w", w=WIN)
        G = sb("G", [P, BODY, D], f32)
        S = sb("S", [P, BODY, P], f32)
        US = sb("US", [P, 2, CW], f32)
        ET = sb("ET", [P, 2, CW], bf16)
        FAR = sb("FAR", [P, 2, P], f32)
        HS = sb("HS", [P, 2, CW], f32)
        WX = sb("WX", [P, 7, D], f32)
        WE = sb("WE", [P, 4 * D], bf16)
        WEM = sb("WEM", [P, 3], f32)
        WEF, WER = HS[:, 0, :], HS[:, 1, :]
        WEP = US[:, :, :].rearrange("p b w -> p (b w)").bitcast(bf16).rearrange("p (c w) -> p c w", w=4 * D)
        ZERO = sb("ZERO", [P, CW], f32)
        ident = sb("ident", [P, P], bf16)
        tri = sb("tri", [P, P], bf16)
        ones = sb("ones", [P, P], bf16)
        row0 = sb("row0", [P, P], bf16)
        iota = sb("iota", [P, WIN], f32)
        iotah = sb("iotah", [P, HI + 1], f16)
        iotap = sb("iotap", [P, 1], f32)
        steps = sb("steps", [P, CIT], f32)
        eps = sb("eps", [P, 1], f32)
        unit1 = sb("unit1", [P, 1], f32)
        cf = sb("cf", [P, 8], f32)
        counts = sb("counts", [P, 4], i32)
        dsti = sb("dsti", [P, CT], i32)
        previ = sb("previ", [P, CT], i32)
        srci = sb("srci", [P, T + BODY], i32)
        seg = sb("seg", [P, CT], f32)
        rel = sb("rel", [P, CT], f32)
        rela = sb("rela", [P, CT], f32)
        nh = sb("nh", [P, CT], f32)
        nl = sb("nl", [P, CT], f32)
        flag = sb("flag", [P, CT], bf16)
        idx = sb("idx", [P, T + BODY], f32)
        s0r = sb("s0r", [P, CT], i32)
        c0r = sb("c0r", [P, CT], i32)
        V4 = sb("V4", [P, CT, 4], bf16)
        AC = sb("AC", [P, CT * 4], f32)
        ACv = AC[:, :].rearrange("p (c w) -> p c w", w=4)
        ti = sb("ti", [P, CT], i32)
        nodes = sb("nodes", [P, CT], f32)
        nodec = sb("nodec", [P, CT], f32)
        inv = sb("inv", [P, CT], f32)
        nlo, nhi, wlo, whi, shi = (sb(n, [P, CT], f32) for n in ("nlo", "nhi", "wlo", "whi", "shi"))
        RX = sb("RX", [P, 1, D], f32)
        shift = sb("shift", [P, 2, LR], f32)
        istage = sb("istage", [P, 2, HALF], u32)
        nstage = sb("nstage", [P, 2, CG], u32)
        stat = sb("stat", [P, 2, LR, 6], f32)
        mv = sb("mv", [P, 2, LR, 2], f32)
        sd = sb("sd", [P, 2, LR], f32)
        rs = sb("rs", [P, 2, LR], f32)

        AREA = 7700
        area = sb("area", [P, AREA], f32)
        at = [0]

        def carve(shape, dt, size):
            n = 1
            for m in shape:
                n *= m
            words = (n * size + 3) // 4
            ap = area[:, at[0]:at[0] + words]
            at[0] += words
            assert at[0] <= AREA, at[0]
            if dt != f32:
                ap = ap.bitcast(dt)
            names_ = "abc"[:len(shape)]
            if len(shape) > 1:
                ap = ap.rearrange(f"p ({' '.join(names_)}) -> p {' '.join(names_)}", **dict(zip(names_[1:], shape[1:])))
            return ap

        SA = carve([BODY, 2 * P], bf16, 2)
        EF = carve([2, HALF, DE], f32, 4)
        EB = carve([2, HALF, EP + 1], bf16, 2)
        EB_END = at[0]
        ECS = carve([2 * CG, len(BLOCKS), EK], bf16, 2)
        ECR = carve([2 * CG, EK], f32, 4)
        TAB = carve([2, HI + 1], f16, 2)
        TABI = carve([2, HI + 1], i32, 4)
        JUNK = carve([2, HI + 1], f16, 2)
        ZH = ZERO[:, :].bitcast(f16)
        SLO = carve([2, HALF * P], i32, 4)
        SLOW = SLO.rearrange("p b w -> p (b w)").bitcast(f16)
        OH = SLOW[:, 0:4 * (HI + 1)].rearrange("p (r w) -> p r w", w=HI + 1)
        LA = SLOW[:, 4 * (HI + 1):4 * (HI + 1 + 2 * P)].rearrange("p (r w) -> p r w", w=2 * P)
        OS = carve([2, HALF * P], f16, 2)
        XG = carve([2, XT * D], f32, 4)
        at[0] = 0
        XL = carve([2, LR * D], f32, 4)
        OL = carve([2, LR * D], f32, 4)
        U1 = carve([2, CW], f32, 4)
        U2 = G[:, 0:8, :].rearrange("p (b j) w -> p b (j w)", b=2)
        at[0] = 0
        XR = carve([2, CW], f32, 4)
        at[0] = EB_END
        SJUNK = carve([SCH], bf16, 2)
        SBELOW = carve([P], f32, 4)
        SOWN = carve([P], f32, 4)
        SEF = carve([HALF, DE], f32, 4)
        SACC = carve([T * P // SCH + 2], f32, 4)
        SPOS = carve([3, HALF], u32, 4)
        SPART = carve([4], i32, 4)
        SPAY = carve([2, HALF], i32, 4)
        DB = UT[:, 0:T * P]

        SG = [pb("segp0"), pb("segp1")]
        LP = [pb("lp0"), pb("lp1")]
        TP = pb("tp")
        HP = [pb("hp0"), pb("hp1")]
        LK = LP + HP
        HPB = [h[:, :].bitcast(bf16) for h in HP]

        names = (
            "ld_dst ld_prev ld_src ld_w const dve tick pool_tick act_tick pe_tick tick_sp pool_chain "
            "order_in order_mm order_known ld_bc ld_sort sort_dve rank_ready sorted "
            "prep_in prep_mm prep_done ut_clear zrow zfill we_ready "
            "idx_ready far row_built s_built summed accum "
            "e_split e_built e_mm e_added ec_ready es_hi es_rest es_mid ecs_full et_mm et_copied "
            "oh_built tab_mm tab_ready os_built look_mm looked a_built a_mm a_added list_in list_mm list_ready "
            "us_staged h_mm h_read ut_zero n_staged sc_staged f_stat f_sd f_out "
            "ln_stat ln_sd shift_ready ln_done act_normed rest_in rest_stat rest_sd rest_done rest_out").split()
        s = {n: sem(n) for n in names}
        gat = [sem(f"gathered{j}") for j in range(BODY)]
        two = lambda n: [sem(f"{n}{b}") for b in (0, 1)]
        ld_ea, ld_lo, st_et, ld_et, ld_u1, ld_u2, st_u, st_h, st_xs, ld_xr = (
            two(n) for n in "ld_ea ld_lo st_et ld_et ld_u1 ld_u2 st_u st_h st_xs ld_xr".split())
        ld_x, st_o = ([sem(f"{n}{q}") for q in range(4)] for n in ("ld_x", "st_o"))
        scat = [sem(f"scattered{j}") for j in range(2 * CG)]
        xg = [sem(f"x_gathered{j}") for j in range(2 * XT)]
        block = ctx.enter_context(nc.Block())

        view = lambda t: t.rearrange("(g j p) c -> g p j c", p=P, j=CG)
        hrows = view(H[1:NSEG + 1, :])
        xsrows = view(XS)
        xspart = XS.rearrange("(g j p) c -> g p j c", p=P, j=XT)
        LN_ROWS = 3 * LIT * 2 * LR * P
        xv = x[0:LN_ROWS, :].rearrange("(g p r) c -> g p (r c)", p=P, r=LR)
        ov = out[0:LN_ROWS, :].rearrange("(g p r) c -> g p (r c)", p=P, r=LR)
        one = lambda ap, g: ap[bass.ds(g, 1)]
        rows4 = lambda ap: ap.rearrange("o p j c -> (o p) j c")
        tile4 = lambda ap: ap.rearrange("p (j c) -> p j c", c=D)

        def seg_steps(e):
            e.wait_ge(s["ec_ready"], 1)
            return e.value_load(counts[0:1, 0:1], min_val=1, max_val=CIT)

        def edge_steps(e):
            e.wait_ge(s["list_ready"], 1)
            return e.value_load(counts[0:1, 1:2], min_val=LIT, max_val=IT)

        SCATTERS = HALF * 5 * 16

        def unsorted(e):
            e.wait_ge(s["order_known"], 1)
            return e.value_load(counts[0:1, 3:4], min_val=0, max_val=T * P)

        @block.sync
        def _(e):
            e.dma_start(dsti[:, 0:T], dst_t).then_inc(s["ld_dst"], 16)
            e.dma_start(previ[:, 0:T], prev_t).then_inc(s["ld_prev"], 16)
            e.dma_start(srci[:, 0:T], src_t).then_inc(s["ld_src"], 16)
            bad = unsorted(e)
            with e.If(bad > 0):
                e.wait_ge(s["ut_clear"], 1)
                e.dma_start(DB.bitcast(i32), dst_rows.partition_broadcast(P)).then_inc(s["ld_bc"], 16)
                e.dma_start(SPT[0:1, :], prev_t[0:1, 0:1]).then_inc(s["ld_bc"], 16)
                with e.Fori(0, 2 * IT) as i:
                    e.dma_start(SEF, one(ea, i).rearrange("o p j w -> (o p) j w")).then_inc(s["ld_sort"], 16)
                    e.wait_ge(s["sorted"], i * SCATTERS + SCATTERS)
                    e.sem_inc(s["tick_sp"], 1)
                e.wait_ge(s["ld_bc"], 32)
                for arr, col, n in ((dsti, SDT, "ld_dst"), (previ, SPT, "ld_prev"), (srci, SST, "ld_src")):
                    e.dma_start(arr[:, 0:T], col.rearrange("(p t) o -> p (t o)", p=P)[:, 0:T]).then_inc(s[n], 16)
            with e.If(bad < 1):
                for n in ("ld_dst", "ld_prev", "ld_src"):
                    e.sem_inc(s[n], 16)
            sea = SEA.rearrange("(h j p) w -> h p j w", p=P, j=HALF)
            e.dma_start(WX[:, :, :], wx).then_inc(s["ld_w"], 16)
            e.wait_ge(s["const"], 1)
            for q in range(len(BLOCKS)):
                e.dma_start(WEF[q * EK:(q + 1) * EK, :], we.rearrange("r k d -> r (k d)")).then_inc(s["ld_w"], 16)
            e.dma_start(WEM[:, :], part_of_block).then_inc(s["ld_w"], 16)
            e.dma_start(H[0:1, :], ZERO[0:1, 0:D]).then_inc(s["zrow"], 16)
            for b in (0, 1):
                e.sem_inc(st_et[b], 16)
                e.sem_inc(st_h[b], 16)
            for q in range(4):
                e.sem_inc(st_o[q], 16)
            e.dma_start(RX[0:LREST, 0, :], x[N - LREST:N, :]).then_inc(s["rest_in"], 16)
            with e.Fori(0, IT) as i:
                for b in (0, 1):
                    h = i * 2 + b
                    e.wait_ge(s["e_split"], h + 1)
                    e.sem_inc(s["tick_sp"], 1)
                    with e.If(bad > 0):
                        e.dma_start(EF[:, b, :, :], one(sea, h).rearrange("o p j w -> (o p) j w")).then_inc(ld_ea[b], 16)
                    with e.If(bad < 1):
                        e.dma_start(EF[:, b, :, :], one(ea, h).rearrange("o p j w -> (o p) j w")).then_inc(ld_ea[b], 16)
            n_s = seg_steps(e)
            with e.Fori(0, CIT) as i:
                with e.If(i < n_s):
                    for b in (0, 1):
                        g = i * 2 + b
                        e.wait_ge(s["et_copied"], g + 3)
                        e.dma_start(ETD[:, bass.ds(g * CW, CW)], ET[0:ES, b, :]).then_inc(st_et[b], 16)
            with e.Fori(0, IT) as i:
                for b in (0, 1):
                    h = i * 2 + b
                    e.wait_ge(s["os_built"], h + 1)
                    e.sem_inc(s["tick_sp"], 1)
                    for rows_, is_ in ((src_rows, bad < 1), (SSR.rearrange("e o -> (e o)"), bad > 0)):
                        with e.If(is_):
                            e.dma_start(SLO[:, b, :], rows_[bass.ds(h * HALF * P, HALF * P)].partition_broadcast(P)).then_inc(ld_lo[b], 16)
            for b in (0, 1):
                e.wait_ge(st_et[b], n_s * 16 + 16)
            e.sem_inc(s["tick_sp"], 1)
            for k in range(4):
                if k == 1:
                    n_e = edge_steps(e)
                if k:
                    e.wait_ge(s["looked"], 4 + T)
                    e.wait_ge(s["a_mm"], 2 + 2 * CIT)
                    for b in (0, 1):
                        e.wait_ge(st_xs[b], n_s * 32 + 16)
                    e.sem_inc(s["tick_sp"], 1)

                    def part(ap, i, q):
                        lo, hi = PARTS[q % 2]
                        return one(ap, i * 2 + ((k - 1) * 2 * LIT + q // 2)).rearrange("o p w -> (o p) w")[:, lo * D:hi * D]

                    def buf(area_, q):
                        lo, hi = PARTS[q % 2]
                        return area_[:, q // 2, lo * D:hi * D]

                    def load_rows(i, q):
                        for n in ("ln_done", "act_normed"):
                            e.wait_ge(s[n], i * 4 + ((k - 1) * 4 * LIT + q + 1))
                        e.dma_start(buf(XL, q), part(xv, i, q)).then_inc(ld_x[q], 16)

                    for q in range(4):
                        load_rows(0, q)
                    with e.Fori(1, LIT) as i:
                        for q in range(4):
                            load_rows(i, q)
                            e.dma_start(part(ov, i - 1, q), buf(OL, q)).then_inc(st_o[q], 16)
                    for q in range(4):
                        for n in ("ln_done", "act_normed"):
                            e.wait_ge(s[n], k * 4 * LIT + q + 1)
                        e.dma_start(part(ov, LIT - 1, q), buf(OL, q)).then_inc(st_o[q], 16)
                    if k == 1:
                        e.wait_ge(s["rest_done"], 1)
                        e.dma_start(out[N - LREST:N, :], RX[0:LREST, 0, :]).then_inc(s["rest_out"], 16)
                    if k == 3:
                        for n in ("ln_done", "act_normed"):
                            e.wait_ge(s[n], 4 + 3 * 4 * LIT)
                if k >= 2:
                    for b in (0, 1):
                        e.wait_ge(st_u[b], n_s * (16 * (k - 1)) + 16)
                if k == 3:
                    e.wait_ge(s["summed"], n_e * (BODY * 3) + (T + BODY))
                e.sem_inc(s["tick_sp"], 1)

                def loads(i, k):
                    for b in (0, 1):
                        g = i * 2 + b
                        m = n_s * (2 * k) + g
                        cols = bass.ds(g * CW, CW)
                        e.wait_ge(s["h_mm"], m + 1)
                        e.dma_start(ET[0:ES, b, :], ETD[:, cols]).then_inc(ld_et[b], 16)
                        if k >= 2:
                            e.dma_start(U1[:, b, :], UD[0][:, cols]).then_inc(ld_u1[b], 16)
                        if k == 3:
                            e.dma_start(U2[:, b, :], UD[1][:, cols]).then_inc(ld_u2[b], 16)
                        yield b
                    if k == 3:
                        for b in (0, 1):
                            g = i * 2 + b
                            e.wait_ge(s["f_stat"], g + 1)
                            e.dma_start(tile4(XR[:, b, :]), rows4(one(xsrows, g))).then_inc(ld_xr[b], 16)

                def store(i, b, k):
                    g = i * 2 + b
                    e.wait_ge(s["h_read"], n_s * (2 * k) + g + 3)
                    e.dma_start(rows4(one(hrows, g)), tile4(HS[:, b, :])).then_inc(st_h[b], 16)

                for b in loads(0, k):
                    pass
                with e.Fori(1, CIT) as i:
                    with e.If(i < n_s):
                        for b in loads(i, k):
                            if k < 3:
                                store(i - 1, b, k)
                if k < 3:
                    for b in (0, 1):
                        store(n_s - 1, b, k)

        @block.gpsimd
        def _(e):
            g = nc.gpsimd
            g.memset(ZERO[:, :], 0.0)
            g.memset(WEF, 0.0)
            g.memset(ET[:, :, :], 0.0).then_inc(s["const"], 1)
            g.memset(ones[:, :], 1.0)
            g.memset(tri[:, :], 1.0)
            g.memset(row0[:, :], 1.0)
            g.memset(ident[:, :], 0.0)
            g.memset(eps[:, :], EPS)
            g.memset(unit1[:, :], 1.0)
            g.memset(EB[:, :, :, DE:DE + 1], 1.0)
            g.iota(iota[:, :], [[1, WIN]], base=0, channel_multiplier=0, allow_small_or_imprecise_dtypes=True)
            g.iota(iotah[:, :], [[1, HI + 1]], base=0, channel_multiplier=0, allow_small_or_imprecise_dtypes=True)
            g.iota(steps[:, :], [[2 * CG * P, CIT]], base=0, channel_multiplier=0, allow_small_or_imprecise_dtypes=True)
            g.iota(ti[:, :], [[P, CT]], base=1, channel_multiplier=1)
            g.iota(iotap[:, :], [[0, 1]], base=0, channel_multiplier=1, allow_small_or_imprecise_dtypes=True).then_inc(s["const"], 1)
            e.wait_ge(s["const"], 2)
            g.affine_select(out=tri[:, :], in_=tri[:, :], compare_op=ALU.is_ge, fill=0.0, base=0, pattern=[[1, P]], channel_multiplier=-1)
            g.affine_select(out=row0[:, :], in_=row0[:, :], compare_op=ALU.is_equal, fill=0.0, base=0, pattern=[[0, P]], channel_multiplier=1)
            g.affine_select(out=ident[:, :], in_=ident[:, :], compare_op=ALU.not_equal, fill=1.0, base=0, pattern=[[1, P]], channel_multiplier=-1).then_inc(s["const"], 1)
            last_node = e.snap(e.to_reg(N - 1))
            last_row = e.snap(e.to_reg(NSEG))
            bad = unsorted(e)
            with e.If(bad > 0):
                with e.Fori(0, 2 * IT) as i:
                    e.wait_ge(s["rank_ready"], i + 1)
                    e.wait_ge(s["ld_sort"], i * 16 + 16)
                    e.sem_inc(s["pool_tick"], 1)
                    for j in range(HALF):
                        for dst_, rows_, w in ((SEA, SEF[:, j, :], 0), (SSR, SPAY[:, 1, j:j + 1], 0), (SDT, SPAY[:, 0, j:j + 1], 1),
                                               (SST, SPAY[:, 1, j:j + 1], 1), (SPT, SPAY[:, 0, j:j + 1], 2)):
                            g.indirect_dma_start(dst_, bass.IndirectOffsetOnAxis(ap=SPOS[:, w, j:j + 1], axis=0), rows_, None,
                                                 bounds_check=last_row, oob_is_err=False).then_inc(s["sorted"], 16)

            def unit(b, u, done, table, last):
                e.wait_ge(s["idx_ready"], u + done[0] + 1)
                e.wait_ge(s["summed"], u * HALF + done[1] + HALF)
                e.sem_inc(s["pool_tick"], 1)
                for j in range(HALF):
                    slot = b * HALF + j
                    g.indirect_dma_start(G[:, slot, :], None, table, bass.IndirectOffsetOnAxis(ap=istage[:, b, j:j + 1], axis=0),
                                         bounds_check=last, oob_is_err=False).then_inc(gat[slot], 16)

            def x_rows(b, n_s):
                with e.Fori(0, CIT) as i:
                    with e.If(i < n_s):
                        for p in (0, 1):
                            e.wait_ge(s["n_staged"], i * 2 + (b * 2 * n_s + (p + 1)))
                            e.wait_ge(st_xs[p], i * 16 + (b * 16 * n_s + 16))
                            e.sem_inc(s["pool_tick"], 1)
                            for j in range(XT):
                                g.indirect_dma_start(XG[:, p, j * D:(j + 1) * D], None, x,
                                                     bass.IndirectOffsetOnAxis(ap=nstage[:, p, j:j + 1], axis=0),
                                                     bounds_check=last_node, oob_is_err=False).then_inc(xg[p * XT + j], 16)

            with e.Fori(0, HALF) as i:
                for b in (0, 1):
                    unit(b, i * 2 + b, (0, 0), x, last_node)
            plink = Chain(e, s["pool_chain"])
            e.wait_ge(s["ld_w"], 16 * (len(BLOCKS) + 2))
            plink(g.tensor_copy(WEP[:, 0, :], WEF))
            plink(g.tensor_tensor(WER, WEF, WEP[:, 0, :], ALU.subtract))
            plink(g.tensor_copy(WEP[:, 1, :], WER))
            plink(g.tensor_tensor(WEP[:, 2, :], WER, WEP[:, 1, :], ALU.subtract))
            for q in range(3):
                plink(g.tensor_scalar(WEP[:, q, :], WEP[:, q, :], WEM[:, q:q + 1], None, ALU.mult))
            plink(g.tensor_tensor(WEP[:, 0, :], WEP[:, 0, :], WEP[:, 1, :], ALU.add))
            g.tensor_tensor(WE[:, :], WEP[:, 0, :], WEP[:, 2, :], ALU.add).then_inc(s["we_ready"], 1)
            e.wait_ge(s["we_ready"], 1)
            n_s = seg_steps(e)
            x_rows(0, n_s)
            with e.Fori(HALF, IT) as i:
                for b in (0, 1):
                    unit(b, i * 2 + b, (0, 0), x, last_node)
            x_rows(1, n_s)
            n_e = edge_steps(e)
            n_z = e.value_load(counts[0:1, 2:3], min_val=0, max_val=CIT)
            e.wait_ge(s["zrow"], 16)
            e.wait_ge(s["zfill"], n_z * 32 + 16)
            for k in range(1, 4):
                for b in (0, 1):
                    e.wait_ge(st_h[b], n_s * (16 * k) + 16)
                e.sem_inc(s["pool_tick"], 1)
                with e.Fori(0, IT) as i:
                    with e.If(i < n_e):
                        for b in (0, 1):
                            unit(b, i * 2 + b, (n_e * (2 * (k - 1)) + 2 * IT, n_e * (BODY * (k - 1)) + T), H, last_row)
            for q in range(4):
                e.wait_ge(st_o[q], 16 * (3 * LIT + 1))
            e.wait_ge(s["rest_out"], 16)
            with e.Fori(0, CIT) as i:
                with e.If(i < n_s):
                    for b in (0, 1):
                        e.wait_ge(s["sc_staged"], i * 2 + b + 1)
                        e.wait_ge(s["f_out"], i * 2 + b + 1)
                        e.sem_inc(s["pool_tick"], 1)
                        for j in range(CG):
                            g.indirect_dma_start(out, bass.IndirectOffsetOnAxis(ap=nstage[:, b, j:j + 1], axis=0),
                                                 HS[:, b, j * D:(j + 1) * D], None,
                                                 bounds_check=last_node, oob_is_err=False).then_inc(scat[b * CG + j], 16)
            for q in range(2 * CG):
                e.wait_ge(scat[q], n_s * 16)
            e.sem_inc(s["pool_tick"], 1)

        @block.scalar
        def _(e):
            a = nc.scalar
            win = [e.alloc_register(f"awin{j}") for j in range(BODY)]

            def stage_indices(b, u, done, arr):
                e.wait_ge(s["summed"], u * HALF + done + HALF)
                a.copy(istage[:, b, :], arr[:, bass.ds(u * HALF, HALF)]).then_inc(s["idx_ready"], 1)

            def accumulate(b, u, done, width, between=None, build=False):
                if b == 0:
                    a.load(win, s0r[0:1, bass.ds(u * HALF, BODY)])
                for j in range(HALF):
                    if between:
                        between(j)
                    bank = SG[(b * HALF + j) % 2]
                    n = u * HALF + done + j
                    w = a.snap(win[b * HALF + j], min_val=0, max_val=NSEG - width)
                    if build:
                        row_distance(u + 1, 1 - b, j)
                    e.wait_ge(s["summed"], n + (BODY + 1))
                    e.wait_ge(s["accum"], n * 2 + 4)
                    first = UT[:, bass.ds(w, 1)]
                    a.activation(first, bank[:, 0:1], ACT.Identity, bias=first).then_inc(s["accum"], 1)
                    if build:
                        row_ones(u + 1, 1 - b, j)
                    a.copy(UT[:, bass.ds(w + 1, width - 1)], bank[:, 1:width]).then_inc(s["accum"], 1)

            def row_distance(u, b, j):
                e.wait_ge(s["row_built"], u * HALF + (j + 1))
                a.activation(FAR[:, (b * HALF + j) % 2, :], iota[:, 0:P], ACT.Abs, bias=rel[:, bass.ds(u * HALF + j, 1)], scale=-1.0).then_inc(s["far"], 1)

            def row_ones(u, b, j):
                e.wait_ge(s["far"], u * HALF + (j + 1))
                a.activation(S[:, b * HALF + j, :], FAR[:, (b * HALF + j) % 2, :], ACT.Relu, bias=unit1[:, 0:1], scale=-1.0).then_inc(s["row_built"], 1)

            e.sem_inc(s["zfill"], 16)
            e.sem_inc(s["row_built"], 2)
            e.sem_inc(s["act_normed"], 4)
            e.sem_inc(s["et_copied"], 2)
            e.sem_inc(s["accum"], 4)
            e.wait_ge(s["const"], 1)

            def clear(lo, hi):
                return a.copy(UT[:, lo * CW:hi * CW].rearrange("p (c w) -> p c w", w=CW), ZERO[:, :].unsqueeze(1).to_broadcast([P, hi - lo, CW]))

            late = -(-(T // 2 + 1) * P // CW)
            clear(0, EARLY).then_inc(s["ut_clear"], 1)
            for b in (0, 1):
                e.sem_inc(st_xs[b], 16)
                e.sem_inc(st_u[b], 16)
            e.wait_ge(s["ld_src"], 32)
            for b in (0, 1):
                stage_indices(b, b, 0, srci)
            clear(EARLY, late).then_inc(s["ut_clear"], 1)
            e.wait_ge(s["prep_done"], 1)
            e.wait_ge(s["ut_clear"], 2)
            for j in range(HALF):
                row_distance(0, 0, j)
                row_ones(0, 0, j)
            with e.Fori(0, HALF) as i:
                for b in (0, 1):
                    accumulate(b, i * 2 + b, 0, P, build=True)
                    stage_indices(b, i * 2 + b + 2, 0, srci)
            clear(late, NSEG // CW).then_inc(s["ut_clear"], 1)
            n_s = seg_steps(e)

            def nodes_in(i, b, p):
                a.copy(nstage[:, p, 0:XT], nodec[:, bass.ds((i * 2 + b) * CG + p * XT, XT)]).then_inc(s["n_staged"], 1)

            def x_out(i, b, p):
                for j in range(XT):
                    e.wait_ge(xg[p * XT + j], i * 16 + (b * 16 * n_s + 16))
                e.dma_start(rows4(one(xspart, (i * 2 + b) * 2 + p)), tile4(XG[:, p, :])).then_inc(st_xs[p], 16)

            def edge_hi(i):
                e.wait_ge(s["et_mm"], i * 2 + 2)
                a.copy(ECS[:, :, 0:3, :], ECv[:, bass.ds(i * 2 * CG, 2 * CG), 0:EK].unsqueeze(2).to_broadcast([P, 2 * CG, 3, EK])).then_inc(s["es_hi"], 1)

            def edge_mid(i):
                e.wait_ge(s["es_rest"], i + 1)
                a.copy(ECS[:, :, 3:5, :], ECR[:, :, :].unsqueeze(2).to_broadcast([P, 2 * CG, 2, EK])).then_inc(s["es_mid"], 1)

            def edge_cols(i, b):
                g = i * 2 + b
                e.wait_ge(s["et_mm"], g + 3)
                e.wait_ge(st_et[b], i * 16 + 16)
                a.copy(ET[0:ES, b, :], HPB[b][0:ES, 0:CW]).then_inc(s["et_copied"], 1)

            for p in (0, 1):
                nodes_in(0, 0, p)
            edge_hi(0)
            edge_mid(0)
            for b in (0, 1):
                edge_cols(0, b)
            with e.Fori(1, CIT) as i:
                with e.If(i < n_s):
                    edge_hi(i)
                    x_out(i - 1, 0, 0)
                    nodes_in(i, 0, 0)
                    edge_mid(i)
                    x_out(i - 1, 0, 1)
                    nodes_in(i, 0, 1)
                    for b in (0, 1):
                        edge_cols(i, b)
            for p in (0, 1):
                x_out(n_s - 1, 0, p)
            e.wait_ge(s["ut_clear"], 3)
            with e.Fori(HALF, IT - 1) as i:
                for b in (0, 1):
                    accumulate(b, i * 2 + b, 0, P, build=True)
                    stage_indices(b, i * 2 + b + 2, 0, srci)
            for b in (0, 1):
                accumulate(b, IT * 2 - 2 + b, 0, P, build=b == 0)

            def stage(i, b, k):
                g = i * 2 + b
                m = n_s * (2 * k) + g
                e.wait_ge(s["h_mm"], m + 1)
                if k in (1, 2):
                    e.wait_ge(st_u[b], n_s * (16 * (k - 1)) + i * 16 + 16)
                a.copy(US[:, b, :], UT[:, bass.ds(g * CW, CW)]).then_inc(s["us_staged"], 1)
                if k < 3:
                    e.wait_ge(s["us_staged"], m + 1)
                    e.sem_inc(s["act_tick"], 1)
                if k in (1, 2):
                    e.dma_start(UD[k - 1][:, bass.ds(g * CW, CW)], US[:, b, :]).then_inc(st_u[b], 16)
                if k < 3:
                    a.copy(UT[:, bass.ds(g * CW, CW)], ZERO[:, :]).then_inc(s["ut_zero"], 1)

            with e.Fori(0, CIT) as i:
                with e.If(i >= n_s):
                    for b in (0, 1):
                        e.dma_start(rows4(one(hrows, i * 2 + b)), tile4(ZERO[:, :])).then_inc(s["zfill"], 16)
            e.wait_ge(s["accum"], 4 + 2 * T)
            for p in (0, 1):
                nodes_in(0, 1, p)
            for b in (0, 1):
                stage(0, b, 0)
            with e.Fori(1, CIT) as i:
                with e.If(i < n_s):
                    for b in (0, 1):
                        stage(i, b, 0)
                    for p in (0, 1):
                        x_out(i - 1, 1, p)
                        nodes_in(i, 1, p)
            for p in (0, 1):
                x_out(n_s - 1, 1, p)
            n_e = edge_steps(e)
            for k in range(1, 4):
                done = n_e * (BODY * (k - 1)) + T
                e.wait_ge(s["summed"], done + BODY)
                e.wait_ge(s["accum"], n_e * (2 * BODY * (k - 1)) + (2 * T + 4))
                for b in (0, 1):
                    stage_indices(b, b, done, idx)

                def unit_sums(i, b, between=None):
                    accumulate(b, i * 2 + b, done, WIN, between)
                    with e.If(i + 1 < n_e):
                        stage_indices(b, i * 2 + b + 2, done, idx)

                def act_norm(m, q):
                    e.wait_ge(s["shift_ready"], m)
                    for r in range(PARTS[q % 2][1] - AR, PARTS[q % 2][1]):
                        c = slice(r * D, (r + 1) * D)
                        last = a.activation(OL[:, q // 2, c], XL[:, q // 2, c], ACT.Identity, bias=shift[:, q // 2, r:r + 1], scale=rs[:, q // 2, r:r + 1])
                    last.then_inc(s["act_normed"], 1)

                def ln_deviation(i, b):
                    def at_tile(j):
                        if j in (0, 3):
                            q = 2 * b + (j > 0)
                            lo, hi = PARTS[q % 2]
                            e.wait_ge(s["ln_stat"], i * 4 + ((k - 1) * 4 * LIT + q + 1))
                            a.activation(sd[:, b, lo:hi], mv[:, b, lo:hi, 1], ACT.Sqrt, bias=eps[:, 0:1]).then_inc(s["ln_sd"], 1)
                            m = i * 4 + ((k - 1) * 4 * LIT + q)
                            if q:
                                act_norm(m, q - 1)
                            else:
                                with e.If(i > 0):
                                    act_norm(m, 3)
                    return at_tile

                if k == 1:
                    e.wait_ge(s["rest_stat"], 1)
                    a.activation(sd[0:LREST, 1, 0:1], mv[0:LREST, 1, 0:1, 1], ACT.Sqrt, bias=eps[0:LREST, 0:1]).then_inc(s["rest_sd"], 1)
                e.wait_ge(s["ut_zero"], n_s * (2 * k))
                with e.Fori(0, LIT) as i:
                    for b in (0, 1):
                        unit_sums(i, b, ln_deviation(i, b))
                act_norm(k * 4 * LIT, 3)
                with e.Fori(LIT, IT) as i:
                    with e.If(i < n_e):
                        for b in (0, 1):
                            unit_sums(i, b)
                            e.sem_inc(s["act_tick"], 1)
                e.wait_ge(s["accum"], n_e * (2 * BODY * k) + (2 * T + 4))
                if k == 3:
                    for b in (0, 1):
                        e.wait_ge(st_u[b], n_s * 32 + 16)

                def deviation(i, b):
                    g = i * 2 + b
                    e.wait_ge(s["f_stat"], g + 3)
                    a.copy(nstage[:, b, :], nodes[:, bass.ds(g * CG, CG)]).then_inc(s["sc_staged"], 1)
                    a.activation(sd[:, b, 0:CG], mv[:, b, 0:CG, 1], ACT.Sqrt, bias=eps[:, 0:1]).then_inc(s["f_sd"], 1)

                for b in (0, 1):
                    stage(0, b, k)
                with e.Fori(1, CIT) as i:
                    with e.If(i < n_s):
                        for b in (0, 1):
                            stage(i, b, k)
                            if k == 3:
                                deviation(i - 1, b)
                if k == 3:
                    for b in (0, 1):
                        deviation(n_s - 1, b)

        @block.vector
        def _(e):
            v = nc.vector
            link = Chain(e, s["dve"])
            for n, c in (("e_added", BODY), ("e_split", 2), ("looked", 4), ("s_built", T), ("h_read", 2), ("os_built", 2), ("f_stat", 2),
                         ("ln_done", 4), ("a_added", 8)):
                e.sem_inc(s[n], c)
            v.memset(EC, 0.0)
            v.memset(AC[:, :], 0.0)
            et = slice(0, T)
            e.wait_ge(s["ld_dst"], 16)
            e.wait_ge(s["ld_prev"], 16)
            link(v.tensor_tensor(flag[:, et], dsti[:, et], previ[:, et], ALU.is_lt))
            e.sem_inc(s["order_in"], 1)
            e.wait_ge(s["order_mm"], 1)
            link(v.reduce_sum(cf[:, 6:7], TP[:, et], AX.X))
            link(v.tensor_copy(counts[:, 3:4], cf[:, 6:7]))
            e.sem_inc(s["order_known"], 1)
            bad = unsorted(e)
            with e.If(bad > 0):
                slink = Chain(e, s["sort_dve"])
                e.wait_ge(s["const"], 2)
                e.wait_ge(s["ld_src"], 16)
                e.wait_ge(s["ld_bc"], 32)
                slink(v.tensor_copy(DB, DB.bitcast(i32)))
                slink(v.tensor_copy(nl[:, et], dsti[:, et]))
                slink(v.tensor_scalar(SBELOW, iota[:, 0:P], iotap[:, 0:1], None, ALU.is_lt))
                with e.Fori(0, 2 * IT) as i:
                    slink.loop(i, 22 * HALF)
                    for j in range(HALF):
                        c = bass.ds(i * HALF + j, 1)
                        d = nl[:, c]
                        own = UT[:, bass.ds((i * HALF + j) * P, P)]
                        for q in range(4):
                            slink(v.tensor_scalar(SJUNK, DB[:, q * SCH:(q + 1) * SCH], d, None, ALU.is_lt, ALU.add, accum_out=SACC[:, q:q + 1]))
                        slink(v.scalar_tensor_tensor(out=SOWN, in0=own, scalar=d, in1=SBELOW, op0=ALU.is_equal, op1=ALU.mult, accum_out=SACC[:, 4:5]))
                        slink(v.tensor_scalar(own, own, -0.5, None, ALU.add))
                        slink(v.reduce_sum(SACC[:, 5:6], SACC[:, 0:5], AX.X))
                        slink(v.tensor_copy(SPOS[:, 0, j:j + 1], SACC[:, 5:6]))
                        slink(v.tensor_copy(SPAY[:, 0, j:j + 1], dsti[:, c]))
                        slink(v.tensor_copy(SPAY[:, 1, j:j + 1], srci[:, c]))
                        for w in (1, 2):
                            slink(v.tensor_scalar(SACC[:, 5:6], SACC[:, 5:6], float(w - 1), None, ALU.add))
                            slink(v.tensor_copy(SPART[:, 0:1], SACC[:, 5:6]))
                            slink(v.tensor_scalar(SPART[:, 1:2], SPART[:, 0:1], 127, None, ALU.bitwise_and))
                            slink(v.tensor_scalar(SPART[:, 2:3], SPART[:, 0:1], 7, None, ALU.logical_shift_right))
                            slink(v.tensor_scalar(SPART[:, 1:2], SPART[:, 1:2], float(T + 1), None, ALU.mult))
                            slink(v.tensor_tensor(SPOS[:, w, j:j + 1], SPART[:, 1:2], SPART[:, 2:3], ALU.add))
                    e.sem_inc(s["rank_ready"], 1)
                    e.wait_ge(s["sorted"], i * SCATTERS + SCATTERS)
                    e.sem_inc(s["tick"], 1)
                slink.end(2 * IT)
                slink(v.memset(UT[:, 0:EARLY * CW], 0.0))
                e.sem_inc(s["tick"], 1)
            e.wait_ge(s["ld_dst"], 32)
            e.wait_ge(s["ld_prev"], 32)
            e.wait_ge(s["const"], 3)

            def ranks(out, base, before):
                link(v.tensor_copy(base, LP[1][:, 0:T]))
                link(v.tensor_tensor_scan(out, base, base, 0.0, ALU.add, ALU.bypass))
                if before is not None:
                    link(v.tensor_copy(before, out[:, T - 1:T]))
                link(v.tensor_tensor(base, out, base, ALU.subtract))
                link(v.tensor_tensor(out, base, LP[0][:, 0:T], ALU.add))
                link(v.tensor_scalar(out, out, -1.0, None, ALU.add))

            def loop_steps(total, step, at_, least):
                n = 2 * CG * P
                link(v.tensor_scalar(cf[:, 2:3], total, -0.5, float(n) / step, ALU.add, ALU.mult))
                link(v.tensor_scalar(JUNKF[:, 0:CIT], steps[:, :], cf[:, 2:3], None, ALU.is_lt, ALU.add, accum_out=cf[:, 3:4]))
                link(v.tensor_scalar(cf[:, 3:4], cf[:, 3:4], float(least), None, ALU.max))
                link(v.tensor_copy(counts[:, at_:at_ + 1], cf[:, 3:4]))

            JUNKF = nlo
            link(v.tensor_tensor(flag[:, et], dsti[:, et], previ[:, et], ALU.not_equal))
            e.sem_inc(s["prep_in"], 1)
            v.tensor_copy(seg[:, et], flag[:, et])
            v.tensor_scalar(s0r[:, et], dsti[:, et], 8, None, ALU.logical_shift_right)
            link(v.tensor_scalar(c0r[:, et], dsti[:, et], 255, None, ALU.bitwise_and))
            v.tensor_tensor(nh[:, et], s0r[:, et], seg[:, et], ALU.mult)
            link(v.tensor_tensor(nl[:, et], c0r[:, et], seg[:, et], ALU.mult))
            e.wait_ge(s["prep_mm"], 1)
            ranks(seg[:, et], rela[:, et], cf[:, 0:1])
            link(v.tensor_tensor(rela[:, et], rela[:, et], HP[0][:, et], ALU.add))
            link(v.tensor_scalar(rela[:, et], rela[:, et], -1.0, None, ALU.add))
            link(v.tensor_copy(s0r[:, et], rela[:, et]))
            link(v.tensor_scalar(c0r[:, et], s0r[:, et], 7, None, ALU.logical_shift_right))
            link(v.tensor_tensor(rel[:, et], seg[:, et], rela[:, et], ALU.subtract))

            def window_places(ranks_, width):
                link(v.tensor_copy(rela[:, et], c0r[:, et]))
                v.tensor_scalar(c0r[:, et], rela[:, et], float(width), None, ALU.mult)
                link(v.tensor_scalar(shi[:, et], rela[:, et], -float(P), None, ALU.mult))
                link(v.tensor_tensor(rela[:, et], ranks_, shi[:, et], ALU.add))

            window_places(seg[:, et], EW)
            loop_steps(cf[:, 0:1], 2 * CG * P, 0, 1)
            link(v.tensor_scalar(counts[:, 2:3], cf[:, 3:4], -1.0, float(CIT), ALU.mult, ALU.add))
            e.sem_inc(s["prep_done"], 1)
            crows = [e.alloc_register(f"ewin{j}") for j in range(BODY)]

            def build_wide(u, j, done):
                e.wait_ge(s["summed"], u * HALF + done + (HALF + 1 + j))
                v.tensor_scalar(SW[:, j, :], iota[:, :], rel[:, bass.ds(u * HALF + j, 1)], None, ALU.is_equal).then_inc(s["s_built"], 1)

            def edge_half(q, h, loads, adds):
                b = q % 2
                if adds and q % 2 == 0:
                    v.load(crows, c0r[0:1, bass.ds((h - 2) * HALF, BODY)])
                e.wait_ge(s["e_mm"], h + 1)
                f = EF[:, b, :, :]
                hi_, mid, lo = (EB[:, b, :, w:w + DE] for w in (0, EW, EW + DE))
                v.tensor_copy(EB[:, b, :, DE + 1], nh[:, bass.ds(h * HALF, HALF)])
                v.tensor_copy(EB[:, b, :, DE + 2], nl[:, bass.ds(h * HALF, HALF)])
                for j in range(HALF):
                    v.tensor_scalar(SA[:, b * HALF + j, :], iotah[:, 0:2 * P], rela[:, bass.ds(h * HALF + j, 1)], None, ALU.is_equal)
                    if adds:
                        add_in(b, h - 2, j)
                    if j == 1:
                        e.wait_ge(ld_ea[b], loads)
                        link.begin(v.tensor_copy(hi_, f))
                    if j == 3:
                        link.sync()
                        link.begin(v.tensor_tensor(f, f, hi_, ALU.subtract))
                    if j == 5:
                        link.sync()
                        link.begin(v.tensor_copy(mid, f))
                link.sync()
                link(v.tensor_tensor(lo, f, mid, ALU.subtract))
                e.sem_inc(s["e_split"], 1)
                e.sem_inc(s["e_built"], 1)

            def add_in(b, h, j):
                c = v.snap(crows[b * HALF + j], min_val=0, max_val=(CT - 2) * EW)
                e.wait_ge(s["e_added"], h * HALF + (BODY + j))
                win = EC[:, bass.ds(c, 2 * EW)]
                v.tensor_tensor(win, win, LP[b][:, j * 2 * EW:(j + 1) * 2 * EW], ALU.add).then_inc(s["e_added"], 1)

            def e_add(b, h):
                if b == 0:
                    v.load(crows, c0r[0:1, bass.ds(h * HALF, BODY)])
                e.wait_ge(s["e_mm"], h + 3)
                for j in range(HALF):
                    add_in(b, h, j)

            def edge_step(i, first):
                for q in range(4):
                    edge_half(q, i * 4 + q, i * 32 + (q // 2) * 16 + 16, q > 1 or not first)

            edge_step(0, True)
            with e.Fori(1, HALF) as i:
                link.loop(i - 1, 16)
                edge_step(i, False)
            link.end(HALF - 1)
            for b in (0, 1):
                e_add(b, 2 * IT - 2 + b)

            e.wait_ge(s["e_added"], BODY + T)
            cnt = ECv[:, :, DE]
            link(v.tensor_scalar(nodec[:, :], ECv[:, :, DE + 1], 256.0, None, ALU.mult))
            link(v.tensor_tensor(nodec[:, :], nodec[:, :], ECv[:, :, DE + 2], ALU.add))
            link(v.tensor_scalar(nodes[:, :], cnt, 0.0, 60000.0, ALU.is_equal, ALU.mult))
            link(v.tensor_tensor(nodes[:, :], nodes[:, :], nodec[:, :], ALU.add))
            link(v.tensor_scalar(nodec[:, :], nodes[:, :], float(N - 1), None, ALU.min))
            link(v.tensor_scalar(inv[:, :], cnt, 1.0, None, ALU.max))
            link(v.reciprocal(inv[:, :], inv[:, :]))
            e.sem_inc(s["ec_ready"], 1)
            n_s = seg_steps(e)
            tw, tv = TABI[:, 0, 0:CT], TABI[:, 1, 0:CT]
            link(v.tensor_copy(tw, nodes[:, :]))
            link(v.tensor_scalar(tv, tw, 127, None, ALU.bitwise_and))
            link(v.tensor_copy(nlo[:, :], tv))
            link(v.tensor_scalar(tv, tw, 7, None, ALU.logical_shift_right))
            link(v.tensor_copy(nhi[:, :], tv))
            link(v.tensor_scalar(tv, ti[:, :], 255, None, ALU.bitwise_and))
            link(v.tensor_copy(wlo[:, :], tv))
            link(v.tensor_scalar(tv, ti[:, :], 0x7F00, None, ALU.bitwise_and))
            link(v.tensor_copy(whi[:, :], tv))
            e.wait_ge(s["ld_src"], 32)
            link(v.tensor_scalar(dsti[:, et], srci[:, et], 7, None, ALU.logical_shift_right))
            link(v.tensor_copy(shi[:, et], dsti[:, et]))
            with e.Fori(0, CIT) as i:
                with e.If(i < n_s):
                    for j in range(2 * CG):
                        c = bass.ds(i * 2 * CG + j, 1)
                        r = j % 4
                        e.wait_ge(s["tab_mm"], i * 2 * CG + (j + 1))
                        v.tensor_scalar(OH[:, r, 0:HI], iotah[:, 0:HI], nhi[:, c], None, ALU.is_equal)
                        v.tensor_scalar(LA[:, r, 0:P], iotah[:, 0:P], nlo[:, c], whi[:, c], ALU.is_equal, ALU.mult)
                        v.tensor_scalar(LA[:, r, P:2 * P], iotah[:, 0:P], nlo[:, c], wlo[:, c], ALU.is_equal, ALU.mult).then_inc(s["oh_built"], 1)
                        if j == 5:
                            e.wait_ge(s["es_hi"], i + 1)
                            v.tensor_tensor(ECR[:, :, :], ECv[:, bass.ds(i * 2 * CG, 2 * CG), 0:EK], ECS[:, :, 0, :], ALU.subtract).then_inc(s["es_rest"], 1)
                        if j == 7:
                            e.wait_ge(s["es_mid"], i + 1)
                            v.tensor_tensor(ECS[:, :, 5, :], ECR[:, :, :], ECS[:, :, 3, :], ALU.subtract).then_inc(s["ecs_full"], 1)
            e.wait_ge(s["tab_mm"], n_s * (2 * CG) + 5)
            link(v.tensor_copy(TABI[:, 0, 0:HI], TP[:, 0:HI]))
            link(v.tensor_scalar(TABI[:, 1, 0:HI], TABI[:, 0, 0:HI], 0x7F00, None, ALU.bitwise_and))
            link(v.tensor_copy(TAB[:, 0, 0:HI], TABI[:, 1, 0:HI]))
            link(v.tensor_scalar(TABI[:, 1, 0:HI], TABI[:, 0, 0:HI], 255, None, ALU.bitwise_and))
            link(v.tensor_copy(TAB[:, 1, 0:HI], TABI[:, 1, 0:HI]))
            e.sem_inc(s["tab_ready"], 1)

            def one_hot_src(i, q, h):
                b = q % 2
                e.wait_ge(ld_lo[b], i * 32 + (q // 2) * 16 + 16)
                link(v.tensor_scalar(SLO[:, b, :], SLO[:, b, :], 127, None, ALU.bitwise_and))
                e.wait_ge(s["look_mm"], h * HALF + HALF)
                v.tensor_scalar(OS[:, b, :], SLO[:, b, :], iotap[:, 0:1], None, ALU.is_equal).then_inc(s["os_built"], 1)

            def select(q, h):
                for j in range(HALF):
                    t = (q * HALF + j) % 2
                    c = bass.ds(h * HALF + j, 1)
                    e.wait_ge(s["look_mm"], h * HALF + (BODY + 1 + j))
                    e.wait_ge(s["looked"], h * HALF + (j + 3))
                    v.scalar_tensor_tensor(out=JUNK[:, t, 0:HI], in0=iotah[:, 0:HI], scalar=shi[:, c], in1=LK[(q * HALF + j) % 4][:, 0:HI],
                                           op0=ALU.is_equal, op1=ALU.mult, accum_out=idx[:, c]).then_inc(s["looked"], 1)

            with e.Fori(0, HALF) as i:
                link.loop(i, 4)
                for q in range(4):
                    one_hot_src(i, q, i * 4 + q)
                    if q:
                        select(q - 1, i * 4 + (q - 1))
                select(3, i * 4 + 3)
            link.end(HALF)

            e.wait_ge(s["looked"], 4 + T)
            v.memset(idx[:, T:CT], 0.0)
            v.memset(seg[:, T:CT], 0.0)
            v.memset(rela[:, T:CT], -1.0)
            link(v.memset(c0r[:, T:CT], 0))
            link(v.tensor_scalar(flag[:, et], idx[:, et], 0.0, None, ALU.is_gt))
            e.sem_inc(s["list_in"], 1)
            for w, arr in ((0, idx), (2, seg)):
                link(v.tensor_copy(dsti[:, :], arr[:, 0:CT]))
                link(v.tensor_scalar(previ[:, :], dsti[:, :], 8, None, ALU.logical_shift_right))
                link(v.tensor_copy(V4[:, :, w], previ[:, :]))
                link(v.tensor_scalar(previ[:, :], dsti[:, :], 255, None, ALU.bitwise_and))
                link(v.tensor_copy(V4[:, :, w + 1], previ[:, :]))
            e.wait_ge(s["list_mm"], 1)
            ranks(wlo[:, et], whi[:, et], cf[:, 1:2])
            link(v.tensor_copy(dsti[:, et], whi[:, et]))
            link(v.tensor_scalar(c0r[:, et], dsti[:, et], 7, None, ALU.logical_shift_right))
            window_places(wlo[:, et], 4)
            link(v.tensor_scalar(rela[:, et], rela[:, et], 1.0, None, ALU.add))
            link(v.tensor_tensor(rela[:, et], rela[:, et], flag[:, et], ALU.mult))
            link(v.tensor_scalar(rela[:, et], rela[:, et], -1.0, None, ALU.add))

            def group_rows(i, k):
                for b in (0, 1):
                    g = i * 2 + b
                    iv = inv[:, bass.ds(g * CG, CG)].unsqueeze(2).to_broadcast([P, CG, D])
                    e.wait_ge(s["h_mm"], g + n_s * (2 * k) + 3)
                    e.wait_ge(st_h[b], n_s * (16 * k) + (i * 16 + 16))
                    v.tensor_tensor(tile4(HS[:, b, :]), tile4(HP[b][:, :]), iv, ALU.mult).then_inc(s["h_read"], 1)

            arow = crows[0:8]
            def list_step(i, build, add):
                if add:
                    v.load(arow, c0r[0:1, bass.ds((i - 1) * 8, 8)])
                for q in (0, 1):
                    e.wait_ge(s["a_mm"], i * 2 + (q + 1))
                    for j in range(4):
                        if build:
                            v_ = v.tensor_scalar(SA[:, q * 4 + j, :], iotah[:, 0:2 * P], rela[:, bass.ds(i * 8 + (q * 4 + j), 1)], None, ALU.is_equal)
                            if j == 3:
                                v_.then_inc(s["a_built"], 1)
                        if add:
                            c = v.snap(arow[q * 4 + j], min_val=0, max_val=(CT - 2) * 4)
                            e.wait_ge(s["a_added"], i * 8 + (q * 4 + j))
                            w = AC[:, bass.ds(c, 8)]
                            v.tensor_tensor(w, w, LP[q][:, j * 8:(j + 1) * 8], ALU.add).then_inc(s["a_added"], 1)

            list_step(0, True, False)
            with e.Fori(1, CIT) as i:
                list_step(i, True, True)
                with e.If(i <= n_s):
                    group_rows(i - 1, 0)
            list_step(CIT, False, True)
            with e.If(n_s > CIT - 1):
                group_rows(CIT - 1, 0)
            e.wait_ge(s["a_added"], 8 + CT)
            link(v.tensor_copy(V4[:, :, :], ACv))
            e.sem_inc(s["list_in"], 1)
            for w, arr in ((0, nlo), (2, nhi)):
                link(v.tensor_scalar(arr[:, :], ACv[:, :, w], 256.0, None, ALU.mult))
                link(v.tensor_tensor(arr[:, :], arr[:, :], ACv[:, :, w + 1], ALU.add))
            e.wait_ge(s["list_mm"], 2)
            link(v.tensor_scalar(wlo[:, :], LP[0][:, 0:CT], 256.0, None, ALU.mult))
            link(v.tensor_tensor(wlo[:, :], wlo[:, :], LP[1][:, 0:CT], ALU.add))
            link(v.tensor_tensor(whi[:, :], nhi[:, :], wlo[:, :], ALU.subtract))
            link(v.tensor_copy(shi[:, :], ti[:, :]))
            link(v.tensor_scalar(shi[:, :], shi[:, :], iotap[:, 0:1], cf[:, 1:2], ALU.subtract, ALU.is_gt))
            link(v.tensor_scalar(shi[:, :], shi[:, :], float(NSEG - WIN), None, ALU.mult))
            link(v.tensor_tensor(wlo[:, :], wlo[:, :], shi[:, :], ALU.add))
            link(v.tensor_scalar(flag[:, :], whi[:, :], float(WIN - 1), None, ALU.is_gt))
            e.sem_inc(s["list_in"], 1)
            e.wait_ge(s["list_mm"], 3)
            link(v.reduce_max(cf[:, 4:5], TP[:, 0:CT], AX.X))
            link(v.tensor_scalar(cf[:, 4:5], cf[:, 4:5], 0.0, None, ALU.is_gt))
            link(v.tensor_copy(shi[:, et], s0r[:, et]))
            for all_, listed in ((idx, nlo), (rel, whi), (shi, wlo), (cf, None)):
                a_, l_ = (all_[:, et], listed[:, et]) if listed is not None else (cf[:, 5:6], cf[:, 1:2])
                if listed is None:
                    link(v.memset(cf[:, 5:6], float(T * P)))
                link(v.tensor_tensor(a_, a_, l_, ALU.subtract))
                link(v.scalar_tensor_tensor(out=a_, in0=a_, scalar=cf[:, 4:5], in1=l_, op0=ALU.mult, op1=ALU.add))
            link(v.tensor_copy(s0r[:, et], shi[:, et]))
            loop_steps(cf[:, 5:6], BODY * P, 1, LIT)
            e.sem_inc(s["list_ready"], 1)
            n_e = edge_steps(e)

            def norm_stats(b, rows, cols, src_):
                for r in range(rows):
                    last = v.bn_stats(stat[cols, b, r, :], src_[cols, b, r * D:(r + 1) * D])
                link(last)
                e.sem_inc(s["tick"], 1)
                for r in range(rows):
                    last = v.bn_aggr(mv[cols, b, r, :], stat[cols, b, r, :])
                return last

            def norm_rows(b, rows, cols, src_, dst_):
                link(v.reciprocal(rs[cols, b, 0:rows], sd[cols, b, 0:rows]))
                for r in range(rows):
                    c = slice(r * D, (r + 1) * D)
                    last = v.tensor_scalar(dst_[cols, b, c], src_[cols, b, c], mv[cols, b, r, 0:1], rs[cols, b, r:r + 1], ALU.subtract, ALU.mult)
                return last

            al = slice(0, P)
            q = slice(0, LREST)
            e.wait_ge(s["rest_in"], 16)
            link(v.bn_stats(stat[q, 1, 0, :], RX[q, 0, :]))
            v.bn_aggr(mv[q, 1, 0, :], stat[q, 1, 0, :]).then_inc(s["rest_stat"], 1)
            e.wait_ge(s["rest_stat"], 1)
            e.wait_ge(s["rest_sd"], 1)
            link(v.reciprocal(rs[q, 1, 0:1], sd[q, 1, 0:1]))
            v.tensor_scalar(RX[q, 0, :], RX[q, 0, :], mv[q, 1, 0, 0:1], rs[q, 1, 0:1], ALU.subtract, ALU.mult).then_inc(s["rest_done"], 1)
            for k in range(1, 4):
                done = n_e * (BODY * (k - 1)) + T

                def norm_before(m, q, tiles=()):
                    b = q // 2
                    lo, hi = PARTS[q % 2]
                    e.wait_ge(s["ln_sd"], m)
                    e.wait_ge(s["act_normed"], m)
                    link(v.reciprocal(rs[:, b, lo:hi], sd[:, b, lo:hi]))
                    v.scalar_tensor_tensor(out=shift[:, b, hi - AR:hi], in0=mv[:, b, hi - AR:hi, 0], scalar=-1.0, in1=rs[:, b, hi - AR:hi],
                                           op0=ALU.mult, op1=ALU.mult).then_inc(s["shift_ready"], 1)
                    for r in range(lo, hi - AR):
                        if tiles:
                            tiles.pop(0)()
                        c = slice(r * D, (r + 1) * D)
                        last = v.tensor_scalar(OL[:, b, c], XL[:, b, c], mv[:, b, r, 0:1], rs[:, b, r:r + 1], ALU.subtract, ALU.mult)
                    last.then_inc(s["ln_done"], 1)

                def ln_step(i, first):
                    for q in range(4):
                        b = q // 2
                        m = i * 4 + ((k - 1) * 4 * LIT + q)
                        lo, hi = PARTS[q % 2]
                        js = range(0, 4) if q % 2 == 0 else range(4, HALF)
                        tiles = [lambda j=j: build_wide(i * 2 + b, j, done) for j in js]
                        tiles.pop(0)()
                        e.wait_ge(ld_x[q], i * 16 + ((k - 1) * LIT + 1) * 16)
                        for r in range(lo, hi):
                            if (r - lo) % 3 == 2 and tiles:
                                tiles.pop(0)()
                            last = v.bn_stats(stat[:, b, r, :], XL[:, b, r * D:(r + 1) * D])
                        link.begin(last)
                        if q or not first:
                            e.wait_ge(st_o[(q - 1) % 4], (i * 16 if q else i * 16 - 16) + ((k - 1) * LIT + 1) * 16)
                            norm_before(m, (q - 1) % 4, tiles)
                        else:
                            link.sync()
                        while tiles:
                            tiles.pop(0)()
                        for r in range(lo, hi):
                            last = v.bn_aggr(mv[:, b, r, :], stat[:, b, r, :])
                        last.then_inc(s["ln_stat"], 1)

                ln_step(0, True)
                with e.Fori(1, LIT) as i:
                    link.loop(i - 1, 8)
                    ln_step(i, False)
                link.end(LIT - 1)
                M = k * 4 * LIT
                e.wait_ge(st_o[3], k * LIT * 16)
                e.wait_ge(s["ln_stat"], M)
                norm_before(M, 3)
                with e.Fori(LIT, IT) as i:
                    with e.If(i < n_e):
                        for b in (0, 1):
                            for j in range(HALF):
                                build_wide(i * 2 + b, j, done)
                if k < 3:
                    with e.Fori(0, CIT) as i:
                        with e.If(i < n_s):
                            group_rows(i, k)
            for b in (0, 1):
                e.wait_ge(st_h[b], n_s * 48 + 16)

            def last_rows(i, peeled):
                for b in (0, 1):
                    g = i * 2 + b
                    iv = inv[:, bass.ds(g * CG, CG)].unsqueeze(2).to_broadcast([P, CG, D])
                    e.wait_ge(s["h_mm"], g + n_s * 6 + 3)
                    if not peeled:
                        for q in range(CG):
                            e.wait_ge(scat[b * CG + q], i * 16)
                    v.tensor_tensor(tile4(HS[:, b, :]), tile4(HP[b][:, :]), iv, ALU.mult).then_inc(s["h_read"], 1)
                    e.wait_ge(s["h_read"], g + n_s * 6 + 3)
                    e.wait_ge(ld_xr[b], i * 16 + 16)
                    link(v.tensor_tensor(HS[:, b, :], HS[:, b, :], XR[:, b, :], ALU.add))
                    norm_stats(b, CG, al, HS).then_inc(s["f_stat"], 1)
                    e.wait_ge(s["f_stat"], g + 3)
                    e.wait_ge(s["f_sd"], g + 1)
                    norm_rows(b, CG, al, HS, HS).then_inc(s["f_out"], 1)

            last_rows(0, True)
            with e.Fori(1, CIT) as i:
                link.loop(i - 1, 6)
                with e.If(i < n_s):
                    last_rows(i, False)

        @block.tensor
        def _(e):
            t = nc.tensor
            for n, c in (("summed", BODY), ("e_mm", 2), ("et_mm", 2), ("tab_mm", 4), ("look_mm", BODY), ("a_mm", 2), ("h_mm", 2)):
                e.sem_inc(s[n], c)
            e.wait_ge(s["const"], 3)
            e.wait_ge(s["order_in"], 1)
            t.matmul(TP[:, 0:T], ones[:, :], flag[:, 0:T], start=True, stop=True).then_inc(s["order_mm"], 1)
            e.wait_ge(s["prep_in"], 1)
            t.matmul(LP[0][:, 0:T], tri[:, :], flag[:, 0:T], start=True, stop=True)
            t.matmul(LP[1][:, 0:T], ones[:, :], flag[:, 0:T], start=True, stop=True)
            t.matmul(HP[0][:, 0:T], row0[:, :], flag[:, 0:T], start=True, stop=True).then_inc(s["prep_mm"], 1)
            e.wait_ge(s["prep_done"], 1)

            def sum_tile(b, u, j, done, step):
                slot = b * HALF + j
                bank = SG[slot % 2]
                n = u * HALF + (0 if done is None else done) + j
                if done is None:
                    e.wait_ge(s["row_built"], n + 3)
                else:
                    e.wait_ge(s["s_built"], n + 1)
                e.wait_ge(s["accum"], n * 2 + 2)
                e.wait_ge(gat[slot], step * 16)
                rhs, width = (S[:, slot, :], P) if done is None else (SW[:, j, :], WIN)
                t.matmul(bank[:, 0:width], G[:, slot, :], rhs, start=True, stop=True).then_inc(s["summed"], 1)

            def sums(b, u, done, step):
                for j in range(HALF):
                    sum_tile(b, u, j, done, step)

            def with_sums(q, j, i):
                b = q // 2
                if q % 2 == j % 2:
                    sum_tile(b, i * 2 + b, j // 2 + (0 if q % 2 == 0 else 4), None, i + 1)

            def edge_sums(i, q, h):
                b = q % 2
                e.wait_ge(s["e_built"], h + 1)
                e.wait_ge(s["e_added"], h * HALF + HALF)
                for j in range(HALF):
                    for w in (0, 1):
                        sa = SA[:, b * HALF + j, w * P:(w + 1) * P]
                        o = LP[b][:, (2 * j + w) * EW:(2 * j + w + 1) * EW]
                        t.matmul(o, sa, EB[:, b, j, 0:EW], start=True, stop=False)
                        t.matmul(o[:, 0:DE], sa, EB[:, b, j, EW:EW + DE], start=False, stop=False)
                        last = t.matmul(o[:, 0:DE], sa, EB[:, b, j, EW + DE:EP], start=False, stop=True)
                    if j == HALF - 1:
                        last.then_inc(s["e_mm"], 1)
                    with_sums(q, j, i)

            with e.Fori(0, HALF) as i:
                for q in range(4):
                    edge_sums(i, q, i * 4 + q)
            n_s = seg_steps(e)
            t.matmul(TP[:, 0:HI], ZH[:, 0:P], ZH[:, 0:HI], start=True, stop=False)
            with e.Fori(0, CIT) as i:
                with e.If(i < n_s):
                    for j in range(2 * CG):
                        r = j % 4
                        e.wait_ge(s["oh_built"], i * 2 * CG + (j + 1))
                        t.matmul(TP[:, 0:HI], LA[:, r, 0:P], OH[:, r, 0:HI], start=False, stop=False)
                        t.matmul(TP[:, 0:HI], LA[:, r, P:2 * P], OH[:, r, 0:HI], start=False, stop=False).then_inc(s["tab_mm"], 1)
                    e.wait_ge(s["ecs_full"], i + 1)
                    for b in (0, 1):
                        g = i * 2 + b
                        e.wait_ge(s["et_copied"], g + 1)
                        for j in range(CG):
                            last = t.transpose(HPB[b][0:ES, j * P:(j + 1) * P], ECS[:, b * CG + j, :, :].rearrange("p c w -> p (c w)"), ident[:, :])
                        last.then_inc(s["et_mm"], 1)
            t.matmul(TP[:, 0:HI], ZH[:, 0:P], ZH[:, 0:HI], start=False, stop=True).then_inc(s["tab_mm"], 1)
            e.wait_ge(s["tab_ready"], 1)

            e.wait_ge(s["et_copied"], n_s * 2 + 2)
            e.sem_inc(s["pe_tick"], 1)

            def look_up(i, q, h):
                e.wait_ge(s["os_built"], h + 3)
                for j in range(HALF):
                    bank = LK[(q * HALF + j) % 4]
                    e.wait_ge(s["looked"], h * HALF + (j + 1))
                    w = OS[:, q % 2, j * P:(j + 1) * P]
                    t.matmul(bank[:, 0:HI], w, TAB[:, 0, 0:HI], start=True, stop=False)
                    t.matmul(bank[:, 0:HI], w, TAB[:, 1, 0:HI], start=False, stop=True).then_inc(s["look_mm"], 1)
                    with_sums(q, j, i + HALF)

            with e.Fori(0, HALF) as i:
                for q in range(4):
                    look_up(i, q, i * 4 + q)
            e.wait_ge(s["looked"], 4 + T)
            e.wait_ge(s["list_in"], 1)
            t.matmul(LP[0][:, 0:T], tri[:, :], flag[:, 0:T], start=True, stop=True)
            t.matmul(LP[1][:, 0:T], ones[:, :], flag[:, 0:T], start=True, stop=True).then_inc(s["list_mm"], 1)
            e.wait_ge(s["we_ready"], 1)
            e.wait_ge(s["et_copied"], n_s * 2 + 2)
            e.sem_inc(s["pe_tick"], 1)

            def products(i, k):
                base = (0, 1, 2, 4)[k]
                for b in (0, 1):
                    g = i * 2 + b
                    m = g + n_s * (2 * k)
                    e.wait_ge(s["h_read"], m + 1)
                    e.wait_ge(ld_et[b], n_s * (16 * k) + (i * 16 + 16))
                    if k >= 2:
                        e.wait_ge(ld_u1[b], n_s * (16 * (k - 2)) + (i * 16 + 16))
                    if k == 3:
                        e.wait_ge(ld_u2[b], i * 16 + 16)
                    e.wait_ge(s["us_staged"], m + 1)
                    ins = [(US, WX[:, base, :])] if k < 2 else [(U1, WX[:, 2, :]), (US, WX[:, 3, :])] if k == 2 else \
                        [(U1, WX[:, 4, :]), (U2, WX[:, 5, :]), (US, WX[:, 6, :])]
                    for j in range(CG):
                        o = HP[b][:, j * P:(j + 1) * P]
                        c = slice(j * P, (j + 1) * P)
                        t.matmul(o, ET[:, b, c], WE[:, k * D:(k + 1) * D], start=True, stop=False)
                        for m_, (u, w) in enumerate(ins):
                            last = t.matmul(o, u[:, b, c], w, start=False, stop=m_ == len(ins) - 1)
                    last.then_inc(s["h_mm"], 1)

            with e.Fori(0, CIT) as i:
                for q in (0, 1):
                    e.wait_ge(s["a_built"], i * 2 + (q + 1))
                    e.wait_ge(s["a_added"], i * 8 + (4 * q + 4))
                    for j in range(4):
                        for w in (0, 1):
                            last = t.matmul(LP[q][:, j * 8 + w * 4:j * 8 + w * 4 + 4], SA[:, q * 4 + j, w * P:(w + 1) * P],
                                            V4[:, bass.ds(i * 8 + (q * 4 + j), 1), :].rearrange("p o c -> p (o c)"), start=True, stop=True)
                    last.then_inc(s["a_mm"], 1)
                with e.If(i < n_s):
                    products(i, 0)
            e.wait_ge(s["list_in"], 2)
            t.matmul(LP[0][:, 0:CT], row0[:, :], V4[:, :, 2], start=True, stop=True)
            t.matmul(LP[1][:, 0:CT], row0[:, :], V4[:, :, 3], start=True, stop=True).then_inc(s["list_mm"], 1)
            e.wait_ge(s["list_in"], 3)
            t.matmul(TP[:, 0:CT], ones[:, :], flag[:, :], start=True, stop=True).then_inc(s["list_mm"], 1)
            n_e = edge_steps(e)
            for k in range(1, 4):
                with e.Fori(0, IT) as i:
                    with e.If(i < n_e):
                        for b in (0, 1):
                            sums(b, i * 2 + b, n_e * (BODY * (k - 1)) + T, n_e * (k - 1) + (i + IT + 1))
                with e.Fori(0, CIT) as i:
                    with e.If(i < n_s):
                        products(i, k)


def kernel(x, src, dst, edge_attr_16, L0_gnn_W0, L0_gnn_b0, L0_gnn_W1, L0_gnn_b1, L0_gnn_W2, L0_gnn_b2, L0_gnn_W3, L0_gnn_b3):
    import numpy as np
    import concourse.bacc as bacc
    from concourse.bass_utils import run_bass_kernel_spmd

    x, src, dst, ea = (np.asarray(v) for v in (x, src, dst, edge_attr_16))
    Ws = [np.asarray(w) for w in (L0_gnn_W0, L0_gnn_W1, L0_gnn_W2, L0_gnn_W3)]
    bs = [np.asarray(b) for b in (L0_gnn_b0, L0_gnn_b1, L0_gnn_b2, L0_gnn_b3)]
    pad = T * P - E
    dst_p = np.pad(dst, (0, pad), constant_values=HI * P)
    prev_p = np.concatenate([np.full(1, -1, dst.dtype), dst_p[:-1]])
    src_p = np.pad(src, (0, pad))
    cols = lambda a: np.ascontiguousarray(a.reshape(T, P).T)
    ea_p = np.pad(ea, ((0, pad), (0, 0))).reshape(2 * IT, HALF, P, DE).transpose(0, 2, 1, 3)
    wx = np.concatenate([w[:-DE] for w in Ws]).reshape(7, D, D).transpose(1, 0, 2)
    we = np.stack([np.concatenate([w[-DE:], b[None]]) for w, b in zip(Ws, bs)], axis=1)
    part_of_block = np.zeros((P, 3), np.float32)
    for q, (_, w) in enumerate(BLOCKS):
        part_of_block[q * EK:(q + 1) * EK, w] = 1
    arrays = {"x": x, "dst_t": cols(dst_p), "prev_t": cols(prev_p), "src_t": cols(src_p), "dst_rows": dst_p, "src_rows": src_p,
              "ea": ea_p, "wx": wx, "we": we, "part_of_block": part_of_block}
    arrays = {k: np.ascontiguousarray(v) for k, v in arrays.items()}
    nc = bacc.Bacc("TRN2", target_bir_lowering=False, num_devices=1)
    args = {k: nc.dram_tensor(k + "_in", v.shape, mybir.dt.from_np(v.dtype), kind="ExternalInput").ap() for k, v in arrays.items()}
    out = nc.dram_tensor("out_rows", (N, D), f32, kind="ExternalOutput").ap()
    gnn_kernel(nc, out=out, **args)
    r = run_bass_kernel_spmd(nc, [{k + "_in": v for k, v in arrays.items()}], core_ids=[0])
    return r.results[0]["out_rows"]
```
